# Optimizing a Trainium2 kernel written in Bass

```python
import numpy as np
import jax
import jax.numpy as jnp

def _softmax(x, axis=-1):
    return jax.nn.softmax(x, axis=axis)

def _gelu(x):
    return jax.nn.gelu(x, approximate=True)

def _silu(x):
    return jax.nn.silu(x)

def _sigmoid(x):
    return jax.nn.sigmoid(x)

def _layernorm(x, axis=-1, eps=1e-05):
    m = jnp.mean(x, axis=axis, keepdims=True)
    v = jnp.var(x, axis=axis, keepdims=True)
    return (x - m) / jnp.sqrt(v + eps)

def _scatter_add(tgt, idx, src, axis=0):
    return tgt.at[idx].add(src)

def _segment_sum(src, seg, n):
    return jax.ops.segment_sum(src, seg, n)
kernel_name = 'mk_gnn_resnorm_d2_gnn_r8_8d16bc'

def setup_inputs(seed: int=0):
    np.random.seed(seed)
    _w = jnp.asarray

    def _rec_inputs():
        import jax
        import jax.numpy as jnp
        _gk = jax.random.key(seed)
        x = -0.0006008 + 1.001 * jax.random.normal(jax.random.fold_in(_gk, 1), (6250, 256), jnp.float32)
        src = jax.random.randint(jax.random.fold_in(_gk, 2), (100000,), 0, 6250, jnp.int32)
        dst = jax.random.randint(jax.random.fold_in(_gk, 3), (100000,), 0, 6250, jnp.int32)
        _o = jnp.argsort(dst, stable=True)
        src = src[_o]
        dst = dst[_o]
        edge_type_8 = jax.random.randint(jax.random.fold_in(_gk, 13), (100000,), 0, 8, jnp.int32)
        return (x, src, dst, edge_type_8)
    x, src, dst, edge_type_8 = _rec_inputs()

    def _L0_gnn_setup():
        import jax, jax.numpy as jnp
        import numpy as np
        N_NODES = 1250
        N_EDGES = 40000
        D = 256

        def _mean_aggregate(x, src, dst, n_nodes):
            msg = x[src]
            summed = jax.ops.segment_sum(msg, dst, num_segments=n_nodes)
            deg = jax.ops.segment_sum(jnp.ones((src.shape[0],), x.dtype), dst, num_segments=n_nodes)
            return summed / jnp.maximum(deg, 1.0)[:, None]

        def _sage_conv(x, src, dst, Wl, bl, Wr, n_nodes):
            mean_nb = _mean_aggregate(x, src, dst, n_nodes)
            return mean_nb @ Wl.T + bl + x @ Wr.T
        key = jax.random.key(seed)
        ks = jax.random.split(key, 9)
        x = jax.random.normal(ks[0], (N_NODES, D), dtype=jnp.float32)
        edge_index = jax.random.randint(ks[1], (2, N_EDGES), 0, N_NODES, dtype=jnp.int32)
        s = 1.0 / np.sqrt(D)
        W1l = jax.random.uniform(ks[2], (D, D), jnp.float32, -s, s)
        b1l = jax.random.uniform(ks[3], (D,), jnp.float32, -s, s)
        W1r = jax.random.uniform(ks[4], (D, D), jnp.float32, -s, s)
        W2l = jax.random.uniform(ks[5], (D, D), jnp.float32, -s, s)
        b2l = jax.random.uniform(ks[6], (D,), jnp.float32, -s, s)
        W2r = jax.random.uniform(ks[7], (D, D), jnp.float32, -s, s)
        return {'x': x, 'edge_index': edge_index, 'W1l': W1l, 'b1l': b1l, 'W1r': W1r, 'W2l': W2l, 'b2l': b2l, 'W2r': W2r}
    _L0_gnn_all = _L0_gnn_setup()
    _L0_gnn_in = {k: v for k, v in _L0_gnn_all.items() if k in ('W1l', 'b1l', 'W1r', 'W2l', 'b2l', 'W2r')}
    del _L0_gnn_all

    def _L1_gnn_setup():
        import jax, jax.numpy as jnp
        import numpy as np
        N_NODES = 2500
        N_EDGES = 40000
        NUM_RELS = 8
        DIM = 256
        BN_EPS = 1e-05
        key = jax.random.key(seed)
        k1, k2, k3, k4, k5 = jax.random.split(key, 5)
        h = jax.random.normal(k1, (N_NODES, DIM), dtype=jnp.float32)
        weight = jax.random.normal(k2, (NUM_RELS, DIM, DIM), dtype=jnp.float32) * 0.05
        gamma = jnp.ones((DIM,), dtype=jnp.float32)
        beta = jnp.zeros((DIM,), dtype=jnp.float32)
        src = jax.random.randint(k3, (N_EDGES,), 0, N_NODES, dtype=jnp.int32)
        dst = jax.random.randint(k4, (N_EDGES,), 0, N_NODES, dtype=jnp.int32)
        rel = jax.random.randint(k5, (N_EDGES,), 0, NUM_RELS, dtype=jnp.int32)
        return {'h': h, 'weight': weight, 'gamma': gamma, 'beta': beta, 'src': src, 'dst': dst, 'rel': rel}
    _L1_gnn_all = _L1_gnn_setup()
    _L1_gnn_in = {k: v for k, v in _L1_gnn_all.items() if k in ('weight', 'gamma', 'beta')}
    del _L1_gnn_all
    return {'x': x, 'src': src, 'dst': dst, 'edge_type_8': edge_type_8, 'L0_gnn_W1l': _L0_gnn_in['W1l'], 'L0_gnn_b1l': _L0_gnn_in['b1l'], 'L0_gnn_W1r': _L0_gnn_in['W1r'], 'L0_gnn_W2l': _L0_gnn_in['W2l'], 'L0_gnn_b2l': _L0_gnn_in['b2l'], 'L0_gnn_W2r': _L0_gnn_in['W2r'], 'L1_gnn_weight': _L1_gnn_in['weight'], 'L1_gnn_gamma': _L1_gnn_in['gamma'], 'L1_gnn_beta': _L1_gnn_in['beta']}

def reference(x, src, dst, edge_type_8, L0_gnn_W1l, L0_gnn_b1l, L0_gnn_W1r, L0_gnn_W2l, L0_gnn_b2l, L0_gnn_W2r, L1_gnn_weight, L1_gnn_gamma, L1_gnn_beta):
    import jax
    import jax.numpy as jnp

    def _L0_gnn_ref(x, edge_index, W1l, b1l, W1r, W2l, b2l, W2r):
        import jax, jax.numpy as jnp
        import numpy as np
        N_NODES = 1250
        N_EDGES = 40000
        D = 256

        def _mean_aggregate(x, src, dst, n_nodes):
            msg = x[src]
            summed = jax.ops.segment_sum(msg, dst, num_segments=n_nodes)
            deg = jax.ops.segment_sum(jnp.ones((src.shape[0],), x.dtype), dst, num_segments=n_nodes)
            return summed / jnp.maximum(deg, 1.0)[:, None]

        def _sage_conv(x, src, dst, Wl, bl, Wr, n_nodes):
            mean_nb = _mean_aggregate(x, src, dst, n_nodes)
            return mean_nb @ Wl.T + bl + x @ Wr.T
        src, dst = (edge_index[0], edge_index[1])
        n = x.shape[0]
        h = jax.nn.relu(_sage_conv(x, src, dst, W1l, b1l, W1r, n))
        h = jax.nn.relu(_sage_conv(h, src, dst, W2l, b2l, W2r, n))
        out = _sage_conv(h, src, dst, W2l, b2l, W2r, n)
        return out

    def _L1_gnn_ref(h, weight, gamma, beta, src, dst, rel):
        import jax, jax.numpy as jnp
        import numpy as np
        N_NODES = 2500
        N_EDGES = 40000
        NUM_RELS = 8
        DIM = 256
        BN_EPS = 1e-05
        all_h = jnp.einsum('ni,rio->nro', h, weight)
        msg = all_h[src, rel]
        agg = jax.ops.segment_sum(msg, dst, num_segments=h.shape[0])
        mean = jnp.mean(agg, axis=0)
        var = jnp.mean(jnp.square(agg - mean), axis=0)
        out = (agg - mean) * jax.lax.rsqrt(var + BN_EPS) * gamma + beta
        return out
    edge_index = jnp.stack([src, dst])
    x = _layernorm(x + _L0_gnn_ref(x, edge_index, L0_gnn_W1l, L0_gnn_b1l, L0_gnn_W1r, L0_gnn_W2l, L0_gnn_b2l, L0_gnn_W2r), axis=-1)
    x = _layernorm(x + _L1_gnn_ref(x, L1_gnn_weight, L1_gnn_gamma, L1_gnn_beta, src, dst, edge_type_8), axis=-1)
    return x

_drawn_inputs = setup_inputs


def setup_inputs(seed=0):
    import zlib

    import numpy as np

    out = dict(_drawn_inputs(seed))
    spreads = {'L1_gnn_gamma': (1.0, 0.2), 'L1_gnn_beta': (0.0, 0.1)}
    factors = {'L0_gnn_b1l': 6.967}
    for name, (base, spread) in spreads.items():
        noise = np.random.default_rng([zlib.crc32(name.encode()), seed]).standard_normal(out[name].shape)
        drawn = base * np.exp(spread * noise) if base else spread * noise
        out[name] = jnp.asarray(drawn.astype(out[name].dtype))
    for name, factor in factors.items():
        out[name] = (out[name] * factor).astype(out[name].dtype)
    return out
```

```python
import numpy as np
import concourse.bass as bass
from concourse import mybir
from contextlib import ExitStack

P = 128
N_NODES = 6250
D = 256
N_EDGES = 100000
RELS = 8
EPS = 1e-5

BLOCKS = -(-N_NODES // P)
LAST_ROWS = N_NODES - (BLOCKS - 1) * P
TILES = -(-N_EDGES // P)
WHOLE_TILES = N_EDGES // P
LAST_EDGES = N_EDGES - WHOLE_TILES * P
VISITS = TILES + BLOCKS - 1
CHUNKS = -(-TILES // P)
BOUNDS = BLOCKS + 1
KC = D // P
PARTS = 3
ROW = PARTS * D
G_SLOTS = 16
M_SLOTS = 32
FULL_RUNS = TILES // G_SLOTS
REST = TILES - FULL_RUNS * G_SLOTS
GROUP = 7
GROUPS = BLOCKS // GROUP
FAR = 1 << 16
SAGE = 3
HALF = VISITS // 2
SOURCE_LOTS = ((0, 0, 4), (0, 4, CHUNKS), (1, 0, 4), (1, 4, CHUNKS))
assert GROUPS * GROUP == BLOCKS and FULL_RUNS % 2 == 0 and VISITS % 2 == 0


def build_gnn(nc, x, src, dst, rel, W1l, b1l, W1r, W2l, b2l, W2r, Wrel, gamma, beta, out):
    fp32, bf16, i32 = mybir.dt.float32, mybir.dt.bfloat16, mybir.dt.int32
    ALU = mybir.AluOpType
    ACT = mybir.ActivationFunctionType
    ds = bass.ds

    tables = [nc.dram_tensor(f"node_table_{n}", [BLOCKS * P, ROW], bf16) for n in range(SAGE)]
    rel_table = nc.dram_tensor("node_relation_table", [BLOCKS * P * RELS, ROW], bf16)

    ctx = ExitStack()
    with ctx:
        def sb(name, shape, dt):
            return ctx.enter_context(nc.sbuf_tensor(name, shape, dt))

        def sem(name):
            return ctx.enter_context(nc.semaphore(name))

        X = sb("X", [P, BLOCKS, D], fp32)
        H = sb("H", [P, BLOCKS, D], fp32)
        G = sb("G", [P, G_SLOTS, ROW], bf16)
        M = sb("M", [P, M_SLOTS, P], bf16)
        rel_dst = sb("rel_dst", [P, VISITS], fp32)
        node_idx = sb("node_idx", [P, CHUNKS * P], i32)
        rel_idx = sb("rel_idx", [P, CHUNKS * P], i32)
        run_idx = sb("run_idx", [P, 2, G_SLOTS], i32)
        stage = sb("stage", [P, 2, RELS, ROW], bf16)
        rest = sb("rest", [P, RELS, D], fp32)
        ident = sb("ident", [P, P], fp32)
        ones = sb("ones", [P, P], fp32)
        zrow = sb("zrow", [1, D], bf16)
        node_iota = sb("node_iota", [P, P], bf16)
        eps = sb("eps", [P, 1], fp32)
        ones_col = sb("ones_col", [P, 1], bf16)
        bounds = sb("bounds", [1, BOUNDS], i32)
        rdeg = sb("rdeg", [P, BLOCKS], fp32)
        mean = sb("mean", [P, D], fp32)
        h_now = sb("h_now", [P, D], fp32)
        x1_now = sb("x1_now", [P, D], fp32)
        turned = sb("turned", [P, 2 * KC, P], fp32)
        x1T = sb("x1T", [P, KC, P], fp32)
        wT = [sb(f"wT{n}", [P, KC, D], fp32) for n in range(4)]
        biases = sb("biases", [1, 2, D], fp32)
        wrel = sb("wrel", [P, KC, RELS * D], fp32)
        stats = sb("stats", [P, GROUP, 6], fp32)
        moments = sb("moments", [P, GROUP, 2], fp32)
        rstd = sb("rstd", [P, GROUP], fp32)
        nbias = sb("nbias", [P, GROUP], fp32)
        gamma_b, beta_b = wT[0][:, 0, :], wT[0][:, 1, :]
        square = rest[:, 0:2, :]
        scale_b = rest[:, 2, :]
        shift = rest[:, 3, :]

        flat = H[:, :, :].rearrange("p b d -> p (b d)")
        taken = [0]

        def scratch(n, dt=fp32):
            at, taken[0] = taken[0], taken[0] + n
            return flat[:, at:at + n].bitcast(dt) if dt != fp32 else flat[:, at:at + n]

        EC = CHUNKS * P
        dst_i, src_i, typ_i = scratch(EC, i32), scratch(EC, i32), scratch(EC, i32)
        dst_f, src_f, typ_f = scratch(EC), scratch(EC), scratch(EC)
        below = scratch(CHUNKS * 64)
        thresholds = scratch(64)
        visit_iota = scratch(VISITS)
        started = scratch(VISITS)
        tile_of = scratch(VISITS)
        tile_iota = scratch(CHUNKS)
        part_iota = scratch(1)
        first_visit = scratch(1)
        minus_block = scratch(P)
        at_tile = [scratch(VISITS), scratch(VISITS)]
        assert taken[0] <= BLOCKS * D

        ring = G[:, :, :].rearrange("p s r -> p (s r)").bitcast(fp32)
        w_in = [ring[:, n * KC * D:(n + 1) * KC * D].rearrange("p (o i) -> p o i", o=KC) for n in range(4)]

        rest_2 = ring[:, 4 * KC * D:4 * KC * D + GROUP * D].rearrange("p (b d) -> p b d", d=D)

        rest_2 = ring[:, 4 * KC * D:4 * KC * D + GROUP * D].rearrange("p (b d) -> p b d", d=D)

        rest_2 = ring[:, 4 * KC * D:4 * KC * D + GROUP * D].rearrange("p (b d) -> p b d", d=D)

        rest_2 = ring[:, 4 * KC * D:4 * KC * D + GROUP * D].rearrange("p (b d) -> p b d", d=D)

        rest_2 = ring[:, 4 * KC * D:4 * KC * D + GROUP * D].rearrange("p (b d) -> p b d", d=D)

        banks = ctx.enter_context(nc.psum_tensor("banks", [P, 8, 512], fp32))
        AGG, TURN, LIN, REL = 0, 2, 3, 4

        pads = sem("pads")
        xpad = sem("xpad")
        made = sem("made")
        edges_in = sem("edges_in")
        consts_in = sem("consts_in")
        norm_in = sem("norm_in")
        weights_in = sem("weights_in")
        x_in = [sem(f"x_in{g}") for g in range(GROUPS)]
        dst_ready = sem("dst_ready")
        sources_ready = sem("sources_ready")
        below_ready = sem("below_ready")
        sources_turned = sem("sources_turned")
        idx_ready = sem("idx_ready")
        counted = sem("counted")
        first_ready = sem("first_ready")
        bounds_ready = sem("bounds_ready")
        started_ready = sem("started_ready")
        spread = sem("spread")
        tile_of_ready = sem("tile_of_ready")
        at_tile_ready = sem("at_tile_ready")
        rel_summed = sem("rel_summed")
        rel_dst_ready = sem("rel_dst_ready")
        weights_turned = sem("weights_turned")
        weights_ready = sem("weights_ready")
        x_hi = sem("x_hi")
        x_rest = sem("x_rest")
        x_mid = sem("x_mid")
        x_low = sem("x_low")
        x_out = [sem("x_out0"), sem("x_out1")]
        g_in = [sem(f"g_in{s}") for s in range(G_SLOTS)]
        run_copied = sem("run_copied")
        arrived = sem("arrived")
        tile_free = sem("tile_free")
        m_ready = sem("m_ready")
        m_free = sem("m_free")
        agg_done = sem("agg_done")
        deg_clamped = sem("deg_clamped")
        deg_ready = sem("deg_ready")
        agg_read = sem("agg_read")
        turn_done = sem("turn_done")
        turn_read = sem("turn_read")
        lin_done = sem("lin_done")
        lin_read = sem("lin_read")
        h_rest = sem("h_rest")
        h_mid = sem("h_mid")
        h_split = sem("h_split")
        table_out = sem("table_out")
        y_stats = sem("y_stats")
        y_moments = sem("y_moments")
        y_root = sem("y_root")
        y_rstd = sem("y_rstd")
        x1_ready = sem("x1_ready")
        x1_kept = sem("x1_kept")
        x1_turned = sem("x1_turned")
        x1T_ready = sem("x1T_ready")
        rel_done = sem("rel_done")
        rel_hi = sem("rel_hi")
        rel_read = sem("rel_read")
        rel_mid = sem("rel_mid")
        rel_split = sem("rel_split")
        rel_out = sem("rel_out")
        first_copied = sem("first_copied")
        first_summed = sem("first_summed")
        shift_ready = sem("shift_ready")
        sq_ready = sem("sq_ready")
        sums_done = sem("sums_done")
        bn_step = sem("bn_step")
        bn_root = sem("bn_root")
        scale_ready = sem("scale_ready")
        offset_added = sem("offset_added")
        scaled = sem("scaled")
        z_ready = sem("z_ready")
        z_stats = sem("z_stats")
        z_moments = sem("z_moments")
        z_root = sem("z_root")
        z_rstd = sem("z_rstd")
        norm_ready = sem("norm_ready")
        normed = sem("normed")
        out_done = [sem("out_done0"), sem("out_done1")]

        def wait_apart(eng, semaphore, value):
            if not isinstance(value, int):
                value = eng.to_reg(value)
            eng.wait_ge(made, 1)
            eng.wait_ge(semaphore, value)

        def slot_before(s, n):
            return 16 * n * (FULL_RUNS + (1 if s < REST else 0))

        def over_blocks(eng, steps, peel=1):
            deep = max(lag for lag, _ in steps)
            first = deep + peel
            for i in range(first):
                for lag, step in steps:
                    if i >= lag:
                        step(i - lag)
            with eng.Fori(first, BLOCKS) as i:
                for lag, step in steps:
                    step(i - lag)
            for i in range(BLOCKS, BLOCKS + deep):
                for lag, step in steps:
                    if i - lag < BLOCKS:
                        step(i - lag)

        def tiles_of(eng, block, between, last):
            lo = eng.value_load(bounds[0:1, ds(block, 1)], min_val=0, max_val=WHOLE_TILES)
            hi = eng.value_load(bounds[0:1, ds(block + 1, 1)], min_val=0, max_val=WHOLE_TILES)
            with eng.If(lo < hi):
                with eng.Fori(lo, hi) as t:
                    between(t)
            last(hi)

        block = ctx.enter_context(nc.Block())

        @block.sync
        def _(sp):
            whole = (CHUNKS - 1) * P * P
            tail = WHOLE_TILES - (CHUNKS - 1) * P
            sp.wait_ge(pads, 3)
            for arr, to in ((src, src_i), (rel, typ_i), (dst, dst_i)):
                to3 = to.rearrange("p (c e) -> p c e", e=P)
                sp.dma_start(to3[:, 0:CHUNKS - 1, :],
                             arr[0:whole].rearrange("(c t e) -> t c e", t=P, e=P)).then_inc(edges_in, 16)
                sp.dma_start(to3[0:tail, CHUNKS - 1, :],
                             arr[whole:whole + tail * P].rearrange("(t e) -> t e", e=P)).then_inc(edges_in, 16)
                sp.dma_start(to3[tail:tail + 1, CHUNKS - 1, 0:LAST_EDGES],
                             arr[whole + tail * P:N_EDGES].rearrange("(t e) -> t e", t=1)).then_inc(edges_in, 16)
            sp.wait_ge(xpad, 1)
            for g in range(GROUPS):
                b0, nb = g * GROUP, GROUP - (g == GROUPS - 1)
                sp.dma_start(X[:, b0:b0 + nb, :], x[b0 * P:(b0 + nb) * P, :].rearrange(
                    "(b p) d -> p b d", p=P)).then_inc(x_in[g], 16)
            sp.dma_start(X[0:LAST_ROWS, BLOCKS - 1, :], x[(BLOCKS - 1) * P:N_NODES, :]).then_inc(x_in[GROUPS - 1], 16)
            for w, to in zip((W1l, W1r, W2l, W2r), w_in):
                sp.dma_start(to, w.rearrange("(o p) i -> p o i", p=P)).then_inc(weights_in, 16)
            for k in range(KC):
                sp.dma_start(wrel[:, k, :].rearrange("p (r o) -> p r o", r=RELS),
                             Wrel[:, k * P:(k + 1) * P, :].rearrange("r p o -> p r o")).then_inc(consts_in, 16)
            sp.dma_start(biases[0:1, 0, :], b1l.rearrange("(a d) -> a d", a=1)).then_inc(consts_in, 16)
            sp.dma_start(biases[0:1, 1, :], b2l.rearrange("(a d) -> a d", a=1)).then_inc(consts_in, 16)

            for g in range(GROUPS):
                sp.wait_ge(x_low, g + 1)
                sp.dma_start(tables[0][g * GROUP * P:(g + 1) * GROUP * P, :].rearrange("(b p) c -> p b c", p=P),
                             stage[:, g % 2, 0:GROUP, :]).then_inc(x_out[g % 2], 16)

            for n in range(SAGE + 1):
                if n == SAGE:
                    for to, v in ((gamma_b, gamma), (beta_b, beta)):
                        sp.dma_start(to, v.rearrange("(a d) -> a d", a=1).to_broadcast([P, D])).then_inc(norm_in, 16)
                with sp.Fori(0, FULL_RUNS) as run:
                    for s in range(G_SLOTS):
                        sp.wait_ge(g_in[s], run * 16 + (slot_before(s, n) + 16))
                        sp.sem_inc(arrived, 1)
                for s in range(REST):
                    sp.wait_ge(g_in[s], slot_before(s, n) + 16 * (FULL_RUNS + 1))
                    sp.sem_inc(arrived, 1)

            for g in range(GROUPS):
                b0, nb = g * GROUP, GROUP - (g == GROUPS - 1)
                sp.wait_ge(normed, GROUP * (g + 1))
                sp.dma_start(out[b0 * P:(b0 + nb) * P, :].rearrange("(b p) d -> p b d", p=P),
                             H[:, b0:b0 + nb, :]).then_inc(out_done[g % 2], 16)
            sp.dma_start(out[(BLOCKS - 1) * P:N_NODES, :], H[0:LAST_ROWS, BLOCKS - 1, :]).then_inc(out_done[1], 16)
            sp.wait_ge(out_done[0], 16 * ((GROUPS + 1) // 2))
            sp.wait_ge(out_done[1], 16 * (GROUPS // 2 + 1))

        @block.gpsimd
        def _(pool):
            gp = nc.gpsimd
            for to, v in ((dst_i, FAR), (src_i, 0), (typ_i, 0)):
                gp.memset(to[:, (CHUNKS - 1) * P:], v).then_inc(pads, 1)
            gp.memset(X[:, BLOCKS - 1, :], 0.0).then_inc(xpad, 1)
            gp.memset(ident[:, :], 0.0).then_inc(made, 1)
            gp.memset(ones[:, :], 1.0).then_inc(made, 1)
            pool.wait_ge(made, 1)
            gp.affine_select(out=ident[:, :], in_=ident[:, :], compare_op=ALU.not_equal, fill=1.0, base=0,
                             pattern=[[-1, P]], channel_multiplier=1).then_inc(made, 1)

            def count(to, width, step, base, by_partition):
                gp.iota(to, pattern=[[step, width]], base=base, channel_multiplier=by_partition,
                        allow_small_or_imprecise_dtypes=True).then_inc(made, 1)

            count(thresholds, 64, P, 0, 0)
            count(visit_iota, VISITS, 1, 0, 0)
            count(tile_iota, CHUNKS, P, -1, 1)
            count(part_iota, 1, 1, 0, 1)
            count(node_iota[:, :], P, 1, -P, 0)
            gp.memset(minus_block, -float(P)).then_inc(made, 1)
            gp.memset(zrow[:, :], 0.0).then_inc(made, 1)
            gp.memset(ones_col[:, :], 1.0).then_inc(made, 1)
            gp.memset(eps[:, :], EPS).then_inc(made, 1)
            pool.wait_ge(idx_ready, 4)

            for n in range(SAGE + 1):
                idx = node_idx if n < SAGE else rel_idx
                table = tables[n] if n < SAGE else rel_table
                copies = n * (FULL_RUNS + 1)
                freed = n * WHOLE_TILES
                if n == 0:
                    pool.wait_ge(weights_turned, 4)
                    pool.wait_ge(x_out[0], 16 * ((GROUPS + 1) // 2))
                    pool.wait_ge(x_out[1], 16 * (GROUPS // 2))
                elif n < SAGE:
                    pool.wait_ge(table_out, 16 * BLOCKS * n)
                else:
                    pool.wait_ge(rel_out, 16 * BLOCKS)

                def gather(parity, s):
                    gp.indirect_dma_start(
                        out=G[:, s, :], out_offset=None, in_=table[:, :],
                        in_offset=bass.IndirectOffsetOnAxis(ap=run_idx[:, parity, s:s + 1], axis=0),
                    ).then_inc(g_in[s], 16)

                def gathers(run, parity, first=False):
                    pool.wait_ge(run_copied, run + (copies + 1))
                    for s in range(G_SLOTS):
                        if not first:
                            wait_apart(pool, tile_free, run * G_SLOTS + (freed + s + 1 - G_SLOTS))
                        if s == G_SLOTS - 1:
                            gp.tensor_copy(run_idx[:, 1 - parity, :],
                                           idx[:, ds((run + 1) * G_SLOTS, G_SLOTS)]).then_inc(run_copied, 1)
                        gather(parity, s)

                gp.tensor_copy(run_idx[:, 0, :], idx[:, 0:G_SLOTS]).then_inc(run_copied, 1)
                gathers(0, 0, first=True)
                gathers(1, 1)
                with pool.Fori(2, FULL_RUNS, 2) as run:
                    gathers(run, 0)
                    gathers(run + 1, 1)
                pool.wait_ge(run_copied, copies + FULL_RUNS + 1)
                for s in range(REST):
                    pool.wait_ge(tile_free, freed + (FULL_RUNS - 1) * G_SLOTS + s + 1)
                    gather(0, s)

            pool.wait_ge(scale_ready, 1)
            for g in range(GROUPS):
                part = H[:, g * GROUP:(g + 1) * GROUP, :]
                gp.tensor_tensor(part, part, scale_b.unsqueeze(1).to_broadcast([P, GROUP, D]),
                                 ALU.mult).then_inc(scaled, 1)

        @block.tensor
        def _(pe):
            te = nc.tensor
            pe.wait_ge(made, 12)
            pe.wait_ge(sources_ready, 2)
            for k, (arr, c0, c1) in enumerate(SOURCE_LOTS):
                for c in range(c0, c1):
                    last = te.transpose(banks[:, REL + k, (c - c0) * P:(c - c0 + 1) * P],
                                        (src_f, typ_f)[arr][:, c * P:(c + 1) * P], ident[:, :])
                last.then_inc(sources_turned, 1)
            pe.wait_ge(below_ready, CHUNKS)
            for c in range(CHUNKS):
                te.matmul(banks[0:BOUNDS, AGG, 0:1], below[:, c * 64:c * 64 + BOUNDS], ones[:, 0:1],
                          start=(c == 0), stop=(c == CHUNKS - 1))
            for c in range(CHUNKS):
                last = te.matmul(banks[0:1, AGG + 1, 0:BOUNDS], ones[:, 0:1], below[:, c * 64:c * 64 + BOUNDS],
                                 start=(c == 0), stop=(c == CHUNKS - 1))
            last.then_inc(counted, 1)
            pe.wait_ge(started_ready, 1)
            for h in range(2):
                last = te.matmul(banks[:, TURN + h, 0:HALF], ones[0:BLOCKS, :],
                                 started[0:BLOCKS, h * HALF:(h + 1) * HALF], start=True, stop=True)
            last.then_inc(spread, 1)
            for h in range(2):
                te.matmul(banks[:, AGG + h, 0:HALF], minus_block[0:BLOCKS, :],
                          started[0:BLOCKS, h * HALF:(h + 1) * HALF], start=True, stop=False)
            for c in range(CHUNKS):
                pe.wait_ge(at_tile_ready, c + 1)
                for h in range(2):
                    last = te.matmul(banks[:, AGG + h, 0:HALF], dst_f[:, c * P:(c + 1) * P],
                                     at_tile[c % 2][:, h * HALF:(h + 1) * HALF], start=False, stop=(c == CHUNKS - 1))
                last.then_inc(rel_summed, 1)
            pe.wait_ge(weights_in, 64)
            pe.wait_ge(idx_ready, 4)
            for n in range(4):
                for k in range(KC):
                    for o in range(KC):
                        last = te.transpose(banks[:, REL + n, (k * KC + o) * P:(k * KC + o + 1) * P],
                                            w_in[n][:, o, k * P:(k + 1) * P], ident[:, :])
                last.then_inc(weights_turned, 1)
            pe.wait_ge(weights_ready, 4)
            pe.wait_ge(consts_in, 16 * 4)
            pe.wait_ge(bounds_ready, 1)
            pe.wait_ge(rel_dst_ready, 1)
            for g in range(GROUPS):
                pe.wait_ge(x_in[g], 16 if g < GROUPS - 1 else 32)
            pe.sem_inc(m_free, M_SLOTS - 1)

            for n in range(SAGE + 1):
                before = n * BLOCKS
                wl, wr = (wT[0], wT[1]) if n == 0 else (wT[2], wT[3])
                bias = biases[0:1, min(n, 1), :]

                def visit(t, b):
                    pe.wait_ge(m_ready, t + b + (n * VISITS + 1))
                    pe.wait_ge(arrived, t + (n * TILES + 1))
                    sel = M[:, (t + b + n * VISITS) & (M_SLOTS - 1), :]
                    slot, bank = t & (G_SLOTS - 1), AGG + ((b + before) & 1)
                    for part in range(PARTS):
                        last = te.matmul(banks[:, bank, 0:D], sel, G[:, slot, part * D:(part + 1) * D],
                                         start=False, stop=False, skip_group_check=True)
                        if part == 0:
                            last.then_inc(m_free, 1)
                            if n == 0:
                                te.matmul(banks[:, bank, D:D + 1], sel, ones_col[:, :],
                                          start=False, stop=False, skip_group_check=True)
                    return last

                def visits(b):
                    if n > 0 or not isinstance(b, int) or b >= 2:
                        pe.wait_ge(agg_read, b + (before - 1))
                    te.matmul(banks[:, AGG + ((b + before) & 1), 0:D], zrow[0:1, 0:P], zrow[0:1, 0:D],
                              start=True, stop=False, skip_group_check=True)
                    tiles_of(te, b, lambda t: visit(t, b).then_inc(tile_free, 1),
                             lambda t: visit(t, b).then_inc(agg_done, 1))

                def turn(j):
                    pe.wait_ge(agg_read, j + (before + 1))
                    if n > 0 or not isinstance(j, int) or j > 0:
                        pe.wait_ge(turn_read, j + before)
                    for k in range(KC):
                        te.transpose(banks[:, TURN, k * P:(k + 1) * P], mean[:, k * P:(k + 1) * P], ident[:, :])
                    for k in range(KC):
                        last = te.transpose(banks[:, TURN, (KC + k) * P:(KC + k + 1) * P],
                                            h_now[:, k * P:(k + 1) * P], ident[:, :])
                    last.then_inc(turn_done, 1)

                def linear(j):
                    pe.wait_ge(turn_read, j + (before + 1))
                    if n > 0 or not isinstance(j, int) or j > 0:
                        pe.wait_ge(lin_read, j + before)
                    te.matmul(banks[:, LIN, 0:D], ones[0:1, :], bias, start=True, stop=False)
                    for k in range(2 * KC):
                        last = te.matmul(banks[:, LIN, 0:D], turned[:, k, :], (wl, wr)[k // KC][:, k % KC, :],
                                         start=False, stop=(k == 2 * KC - 1))
                    last.then_inc(lin_done, 1)

                def turn_x1(j):
                    pe.wait_ge(x1_ready, j + 1)
                    if not isinstance(j, int) or j > 0:
                        pe.wait_ge(rel_read, j)
                    for k in range(KC):
                        last = te.transpose(banks[:, REL + 3, k * P:(k + 1) * P], x1_now[:, k * P:(k + 1) * P], ident[:, :])
                    last.then_inc(x1_turned, 1)

                def relations(j):
                    pe.wait_ge(x1T_ready, j + 1)
                    for q in range(4):
                        for k in range(KC):
                            last = te.matmul(banks[:, REL + q, :], x1T[:, k, :], wrel[:, k, q * 512:(q + 1) * 512],
                                             start=(k == 0), stop=(k == KC - 1))
                    last.then_inc(rel_done, 1)

                def sum_first(j):
                    if isinstance(j, int) and j == 0:
                        pe.wait_ge(first_copied, 1)
                        te.matmul(banks[:, TURN, 0:D], ones[:, :], mean[:, :], start=True,
                                  stop=True).then_inc(first_summed, 1)

                def sums(j):
                    rows = LAST_ROWS if isinstance(j, int) and j == BLOCKS - 1 else P
                    pe.wait_ge(agg_read, j + (before + 1))
                    pe.wait_ge(sq_ready, j + 1)
                    te.matmul(banks[:, LIN, 0:D], ones[0:rows, :], H[0:rows, j, :],
                              start=False, stop=False, skip_group_check=True)
                    te.matmul(banks[:, LIN, D:2 * D], ones[0:rows, :], square[0:rows, j & 1, :],
                              start=False, stop=False, skip_group_check=True).then_inc(sums_done, 1)

                if n < SAGE - 1:
                    over_blocks(pe, [(0, visits), (1, turn), (1, linear)])
                elif n == SAGE - 1:
                    over_blocks(pe, [(0, visits), (1, turn), (2, turn_x1), (1, linear), (2, relations)])
                else:
                    pe.wait_ge(lin_read, SAGE * BLOCKS)
                    te.matmul(banks[:, LIN, 0:2 * D], zrow[0:1, 0:P], zrow[0:1, 0:1].to_broadcast([1, 2 * D]),
                              start=True, stop=False, skip_group_check=True)
                    over_blocks(pe, [(0, visits), (1, sum_first), (2, sums)])

        @block.vector
        def _(dve):
            ve = nc.vector
            dve.wait_ge(edges_in, 16 * 9)
            ve.tensor_copy(src_f, src_i).then_inc(sources_ready, 1)
            ve.scalar_tensor_tensor(out=typ_f, in0=src_i, scalar=float(RELS), in1=typ_i,
                                    op0=ALU.mult, op1=ALU.add).then_inc(sources_ready, 1)
            ve.tensor_copy(dst_f, dst_i).then_inc(dst_ready, 1)
            dve.wait_ge(made, 12)
            dve.wait_ge(dst_ready, 1)
            for c in range(CHUNKS):
                ve.tensor_scalar(below[:, c * 64:(c + 1) * 64], thresholds, dst_f[:, (c + 1) * P - 1:(c + 1) * P],
                                 None, ALU.is_gt).then_inc(below_ready, 1)
            for k, (arr, c0, c1) in enumerate(SOURCE_LOTS):
                dve.wait_ge(sources_turned, k + 1)
                ve.tensor_copy((node_idx, rel_idx)[arr][:, c0 * P:c1 * P],
                               banks[:, REL + k, 0:(c1 - c0) * P]).then_inc(idx_ready, 1)

            for g in range(GROUPS):
                part = stage[:, g % 2, 0:GROUP, :]
                left = (rest[:, 0:GROUP, :], rest_2)[g % 2]
                dve.wait_ge(x_hi, g + 1)
                ve.tensor_tensor(left, X[:, g * GROUP:(g + 1) * GROUP, :], part[:, :, 0:D],
                                 ALU.subtract).then_inc(x_rest, 1)
                if g == 0:
                    dve.wait_ge(counted, 1)
                    ve.tensor_tensor(first_visit[0:BOUNDS, :], banks[0:BOUNDS, AGG, 0:1], part_iota[0:BOUNDS, :],
                                     ALU.add).then_inc(first_ready, 1)
                    ve.tensor_copy(bounds[0:1, :], banks[0:1, AGG + 1, 0:BOUNDS]).then_inc(bounds_ready, 1)
                    dve.wait_ge(first_ready, 1)
                    ve.tensor_scalar(started[0:BLOCKS, :], visit_iota[0:BLOCKS, :], first_visit[0:BLOCKS, :],
                                     None, ALU.is_ge).then_inc(started_ready, 1)
                dve.wait_ge(x_mid, g + 1)
                dve.wait_ge(x_rest, g + 1)
                ve.tensor_tensor(part[:, :, 2 * D:3 * D], left, part[:, :, D:2 * D],
                                 ALU.subtract).then_inc(x_low, 1)

            dve.wait_ge(spread, 1)
            for h in range(2):
                ve.tensor_tensor(tile_of[:, h * HALF:(h + 1) * HALF], visit_iota[:, h * HALF:(h + 1) * HALF],
                                 banks[:, TURN + h, 0:HALF], ALU.subtract).then_inc(tile_of_ready, 1)
            dve.wait_ge(tile_of_ready, 2)
            for c in range(CHUNKS):
                if c >= 2:
                    dve.wait_ge(rel_summed, c - 1)
                ve.tensor_scalar(at_tile[c % 2], tile_of, tile_iota[:, c:c + 1], None,
                                 ALU.is_equal).then_inc(at_tile_ready, 1)
            dve.wait_ge(rel_summed, CHUNKS)
            for h in range(2):
                last = ve.tensor_copy(rel_dst[:, h * HALF:(h + 1) * HALF], banks[:, AGG + h, 0:HALF])
            last.then_inc(rel_dst_ready, 1)
            dve.wait_ge(rel_dst_ready, 1)
            dve.wait_ge(bounds_ready, 1)

            for n in range(SAGE + 1):
                before = n * BLOCKS

                def select(t, b):
                    dve.wait_ge(m_free, t + b + (n * VISITS + 1))
                    ve.tensor_scalar(M[:, (t + b + n * VISITS) & (M_SLOTS - 1), :], node_iota[:, :],
                                     rel_dst[:, ds(t + b, 1)], None, ALU.is_equal).then_inc(m_ready, 1)

                def selections(b):
                    tiles_of(ve, b, lambda t: select(t, b), lambda t: select(t, b))

                def degrees(j):
                    dve.wait_ge(agg_done, j + 1)
                    ve.tensor_scalar(rdeg[:, ds(j, 1)], banks[:, AGG + (j & 1), D:D + 1], 1.0, None,
                                     ALU.max).then_inc(deg_clamped, 1)
                    wait_apart(dve, deg_clamped, j + 1)
                    ve.reciprocal(rdeg[:, ds(j, 1)], rdeg[:, ds(j, 1)]).then_inc(deg_ready, 1)

                def split_h(j):
                    row = stage[:, 0, j & 3, :]
                    dve.wait_ge(lin_read, j + (before + 1))
                    if n > 0 or not isinstance(j, int) or j > 0:
                        dve.wait_ge(h_split, j + before)
                    ve.tensor_tensor(rest[:, 0, :], H[:, j, :], row[:, 0:D], ALU.subtract).then_inc(h_rest, 1)
                    dve.wait_ge(h_rest, j + (before + 1))
                    ve.tensor_copy(row[:, D:2 * D], rest[:, 0, :]).then_inc(h_mid, 1)
                    dve.wait_ge(h_mid, j + (before + 1))
                    ve.tensor_tensor(row[:, 2 * D:3 * D], rest[:, 0, :], row[:, D:2 * D],
                                     ALU.subtract).then_inc(h_split, 1)

                def layernorm(j):
                    dve.wait_ge(lin_done, j + (before + 1))
                    if not isinstance(j, int) or j > 0:
                        dve.wait_ge(x1_turned, j)
                        dve.wait_ge(x1_kept, j)
                    ve.tensor_tensor(x1_now[:, :], banks[:, LIN, 0:D], X[:, j, :], ALU.add).then_inc(lin_read, 1)
                    dve.wait_ge(lin_read, j + (before + 1))
                    ve.bn_stats(stats[:, 0, :], x1_now[:, :]).then_inc(y_stats, 1)
                    wait_apart(dve, y_stats, j + 1)
                    ve.bn_aggr(moments[:, 0, :], stats[:, 0, :]).then_inc(y_moments, 1)
                    dve.wait_ge(y_root, j + 1)
                    ve.reciprocal(rstd[:, 0:1], rstd[:, 0:1]).then_inc(y_rstd, 1)
                    dve.wait_ge(y_rstd, j + 1)
                    ve.tensor_scalar(x1_now[:, :], x1_now[:, :], moments[:, 0, 0:1], rstd[:, 0:1], ALU.subtract,
                                     ALU.mult).then_inc(x1_ready, 1)

                def split_relations(j):
                    part = stage[:, j & 1, :, :]
                    values = banks[:, REL:REL + 4, :].rearrange("p q (r d) -> p (q r) d", r=2)
                    dve.wait_ge(rel_hi, j + 1)
                    if not isinstance(j, int) or j > 0:
                        dve.wait_ge(rel_split, j)
                    ve.tensor_tensor(rest[:, :, :], values, part[:, :, 0:D], ALU.subtract).then_inc(rel_read, 1)
                    dve.wait_ge(rel_read, j + 1)
                    ve.tensor_copy(part[:, :, D:2 * D], rest[:, :, :]).then_inc(rel_mid, 1)
                    dve.wait_ge(rel_mid, j + 1)
                    ve.tensor_tensor(part[:, :, 2 * D:3 * D], rest[:, :, :], part[:, :, D:2 * D],
                                     ALU.subtract).then_inc(rel_split, 1)

                def deviations(j):
                    bank = AGG + ((j + before) & 1)
                    dve.wait_ge(agg_done, j + (before + 1))
                    if isinstance(j, int) and j == 0:
                        ve.tensor_copy(mean[:, :], banks[:, bank, 0:D]).then_inc(first_copied, 1)
                        dve.wait_ge(first_summed, 1)
                        ve.tensor_scalar(shift, banks[:, TURN, 0:D], 1.0 / P, None, ALU.mult).then_inc(shift_ready, 1)
                        dve.wait_ge(shift_ready, 1)
                    ve.tensor_tensor(H[:, j, :], banks[:, bank, 0:D], shift, ALU.subtract).then_inc(agg_read, 1)

                if n == 0:
                    over_blocks(dve, [(0, selections), (1, degrees), (2, split_h)])
                elif n < SAGE - 1:
                    over_blocks(dve, [(0, selections), (2, split_h)])
                elif n == SAGE - 1:
                    over_blocks(dve, [(0, selections), (2, layernorm), (3, split_relations)])
                else:
                    over_blocks(dve, [(0, selections), (1, deviations)])

            steps = [0]

            def then(ins):
                steps[0] += 1
                ins.then_inc(bn_step, 1)
                dve.wait_ge(bn_step, steps[0])

            dve.wait_ge(norm_in, 32)
            dve.wait_ge(sums_done, BLOCKS)
            then(ve.tensor_scalar(mean[:, :], banks[:, LIN, 0:D], 1.0 / N_NODES, None, ALU.mult))
            then(ve.tensor_tensor(shift, mean[:, :], mean[:, :], ALU.mult))
            then(ve.scalar_tensor_tensor(out=scale_b, in0=banks[:, LIN, D:2 * D], scalar=1.0 / N_NODES,
                                         in1=shift, op0=ALU.mult, op1=ALU.subtract))
            dve.wait_ge(bn_root, 1)
            then(ve.reciprocal(scale_b, scale_b))
            then(ve.tensor_tensor(scale_b, scale_b, gamma_b, ALU.mult))
            ve.tensor_tensor(mean[:, :], mean[:, :], scale_b, ALU.mult).then_inc(scale_ready, 1)
            dve.wait_ge(scale_ready, 1)
            then(ve.tensor_tensor(shift, beta_b, mean[:, :], ALU.subtract))
            for g in range(GROUPS):
                b0 = g * GROUP
                xg, zg = X[:, b0:b0 + GROUP, :], H[:, b0:b0 + GROUP, :]
                ve.tensor_tensor(xg, xg, shift.unsqueeze(1).to_broadcast([P, GROUP, D]),
                                 ALU.add).then_inc(offset_added, 1)
                dve.wait_ge(offset_added, g + 1)
                dve.wait_ge(scaled, g + 1)
                ve.tensor_tensor(zg, zg, xg, ALU.add).then_inc(z_ready, 1)
                dve.wait_ge(z_ready, g + 1)
                if g > 0:
                    dve.wait_ge(normed, b0)
                for i in range(GROUP):
                    ve.bn_stats(stats[:, i, :], H[:, b0 + i, :]).then_inc(z_stats, 1)
                dve.wait_ge(z_stats, b0 + GROUP)
                for i in range(GROUP):
                    ve.bn_aggr(moments[:, i, :], stats[:, i, :]).then_inc(z_moments, 1)
                dve.wait_ge(z_root, g + 1)
                ve.reciprocal(rstd[:, :], rstd[:, :]).then_inc(z_rstd, 1)
                dve.wait_ge(z_rstd, g + 1)
                ve.scalar_tensor_tensor(out=nbias[:, :], in0=moments[:, :, 0], scalar=-1.0, in1=rstd[:, :],
                                        op0=ALU.mult, op1=ALU.mult).then_inc(norm_ready, 1)

        @block.scalar
        def _(act):
            sc = nc.scalar
            def x_first(g):
                act.wait_ge(x_in[g], 16 if g < GROUPS - 1 else 32)
                if g >= 2:
                    act.wait_ge(x_out[g % 2], 16 * (g // 2))
                sc.activation(stage[:, g % 2, 0:GROUP, 0:D], X[:, g * GROUP:(g + 1) * GROUP, :],
                              ACT.Copy).then_inc(x_hi, 1)

            x_first(0)
            for g in range(GROUPS):
                if g + 1 < GROUPS:
                    x_first(g + 1)
                act.wait_ge(x_rest, g + 1)
                sc.activation(stage[:, g % 2, 0:GROUP, D:2 * D], (rest[:, 0:GROUP, :], rest_2)[g % 2],
                              ACT.Copy).then_inc(x_mid, 1)
            for n in range(4):
                act.wait_ge(weights_turned, n + 1)
                sc.activation(wT[n][:, :, :], banks[:, REL + n, :].rearrange("p (k o) -> p k o", k=KC),
                              ACT.Copy).then_inc(weights_ready, 1)
            act.wait_ge(x_out[0], 16 * ((GROUPS + 1) // 2))
            act.wait_ge(x_out[1], 16 * (GROUPS // 2))

            for n in range(SAGE + 1):
                before = n * BLOCKS

                def means(j):
                    act.wait_ge(agg_done, j + (before + 1))
                    if n == 0:
                        act.wait_ge(deg_ready, j + 1)
                    if n > 0 or not isinstance(j, int) or j > 0:
                        act.wait_ge(turn_done, j + before)
                    sc.activation(h_now[:, :], (X if n == 0 else H)[:, j, :], ACT.Copy)
                    sc.activation(mean[:, :], banks[:, AGG + ((j + before) & 1), 0:D], ACT.Copy,
                                  scale=rdeg[:, ds(j, 1)]).then_inc(agg_read, 1)

                def take_turned(j):
                    act.wait_ge(turn_done, j + (before + 1))
                    if n > 0 or not isinstance(j, int) or j > 0:
                        act.wait_ge(lin_done, j + before)
                    sc.activation(turned[:, :, :], banks[:, TURN, :].rearrange("p (k m) -> p k m", m=P),
                                  ACT.Copy).then_inc(turn_read, 1)

                def hidden(j):
                    wait_apart(act, lin_done, j + (before + 1))
                    sc.activation(H[:, j, :], banks[:, LIN, 0:D], ACT.Relu)
                    sc.activation(stage[:, 0, j & 3, 0:D], banks[:, LIN, 0:D], ACT.Relu).then_inc(lin_read, 1)

                def write_h(j):
                    act.wait_ge(h_split, j + (before + 1))
                    if n > 0 or not isinstance(j, int) or j > 0:
                        act.wait_ge(table_out, (j + before) * 16)
                    act.dma_start(tables[n + 1][ds(j * P, P), :], stage[:, 0, j & 3, :]).then_inc(table_out, 16)

                def root(j):
                    act.wait_ge(y_moments, j + 1)
                    if not isinstance(j, int) or j > 0:
                        act.wait_ge(x1_ready, j)
                    sc.activation(rstd[:, 0:1], moments[:, 0, 1:2], ACT.Sqrt, bias=eps[:, :]).then_inc(y_root, 1)

                def keep_x1(j):
                    act.wait_ge(x1_ready, j + 1)
                    sc.activation(X[:, j, :], x1_now[:, :], ACT.Copy).then_inc(x1_kept, 1)

                def take_x1T(j):
                    act.wait_ge(x1_turned, j + 1)
                    if not isinstance(j, int) or j > 0:
                        act.wait_ge(rel_done, j)
                    sc.activation(x1T[:, :, :], banks[:, REL + 3, 0:D].rearrange("p (k m) -> p k m", m=P),
                                  ACT.Copy).then_inc(x1T_ready, 1)

                def first_part(j):
                    act.wait_ge(rel_done, j + 1)
                    sc.activation(stage[:, j & 1, :, 0:D],
                                  banks[:, REL:REL + 4, :].rearrange("p q (r d) -> p (q r) d", r=2),
                                  ACT.Copy).then_inc(rel_hi, 1)

                def write_relations(j):
                    act.wait_ge(rel_split, j + 1)
                    if not isinstance(j, int) or j > 0:
                        act.wait_ge(rel_out, j * 16)
                    act.dma_start(rel_table[ds(j * P * RELS, P * RELS), :].rearrange("(p r) c -> p (r c)", r=RELS),
                                  stage[:, j & 1, :, :].rearrange("p r c -> p (r c)")).then_inc(rel_out, 16)

                def squares(j):
                    act.wait_ge(agg_read, j + (before + 1))
                    if not isinstance(j, int) or j >= 2:
                        act.wait_ge(sums_done, j - 1)
                    sc.activation(square[:, j & 1, :], H[:, j, :], ACT.Square).then_inc(sq_ready, 1)

                if n < SAGE - 1:
                    over_blocks(act, [(1, means), (3, write_h), (1, take_turned), (1, hidden)])
                elif n == SAGE - 1:
                    act.wait_ge(table_out, 16 * BLOCKS * (SAGE - 1))
                    over_blocks(act, [(1, means), (4, write_relations), (3, first_part), (2, root), (1, take_turned), (2, keep_x1), (2, take_x1T)])
                else:
                    over_blocks(act, [(2, squares)], peel=2)

            act.wait_ge(bn_step, 3)
            sc.activation(scale_b, scale_b, ACT.Sqrt, bias=eps[:, :]).then_inc(bn_root, 1)
            for g in range(GROUPS):
                act.wait_ge(z_moments, (g + 1) * GROUP)
                sc.activation(rstd[:, :], moments[:, :, 1], ACT.Sqrt, bias=eps[:, :]).then_inc(z_root, 1)
                act.wait_ge(norm_ready, g + 1)
                for i in range(GROUP):
                    zb = H[:, g * GROUP + i, :]
                    sc.activation(zb, zb, ACT.Identity, scale=rstd[:, i:i + 1],
                                  bias=nbias[:, i:i + 1]).then_inc(normed, 1)


_INS = ['x', 'src', 'dst', 'edge_type_8', 'L0_gnn_W1l', 'L0_gnn_b1l', 'L0_gnn_W1r', 'L0_gnn_W2l', 'L0_gnn_b2l',
        'L0_gnn_W2r', 'L1_gnn_weight', 'L1_gnn_gamma', 'L1_gnn_beta']
_OUT = ((N_NODES, D), 'float32')


def kernel(**inputs):
    import concourse.bacc as _bacc
    from concourse.bass_utils import run_bass_kernel_spmd as _run

    nc = _bacc.Bacc("TRN2", target_bir_lowering=False, num_devices=1)
    arrays, args = {}, []
    for name in _INS:
        a = np.ascontiguousarray(inputs[name])
        arrays[f"in_{name}"] = a
        args.append(nc.dram_tensor(f"in_{name}", a.shape, mybir.dt.from_np(a.dtype), kind="ExternalInput").ap())
    args.append(nc.dram_tensor("result", _OUT[0], mybir.dt.from_np(np.dtype(_OUT[1])), kind="ExternalOutput").ap())
    build_gnn(nc, *args)
    return _run(nc, [arrays], core_ids=[0]).results[0]["result"]
```

```python
import numpy as np
import concourse.bass as bass
from concourse import mybir
from contextlib import ExitStack

P = 128
N_NODES = 6250
D = 256
N_EDGES = 100000
RELS = 8
EPS = 1e-5

BLOCKS = -(-N_NODES // P)
LAST_ROWS = N_NODES - (BLOCKS - 1) * P
WHOLE_TILES = N_EDGES // P
LAST_EDGES = N_EDGES - WHOLE_TILES * P
QUAD = 4
RUN = 4
G_SLOTS = QUAD * RUN
RUNS = -(-N_EDGES // (P * G_SLOTS))
QUADS = RUNS * RUN
TILES = QUADS * QUAD
VISITS = QUADS + BLOCKS - 1
CHUNKS = -(-TILES // P)
BOUNDS = BLOCKS + 1
KC = D // P
PARTS = 3
ROW = PARTS * D
GROUP = 7
GROUPS = BLOCKS // GROUP
FAR = 1 << 16
SAGE = 3
VT = VISITS * QUAD
HALF = VT // 2
SOURCE_LOTS = ((0, 0, 4), (0, 4, CHUNKS), (1, 0, 4), (1, 4, CHUNKS))
assert GROUPS * GROUP == BLOCKS and RUNS % 2 == 1 and HALF <= 512 and QUADS * QUAD * P > N_EDGES


def build_gnn(nc, x, src, dst, rel, W1l, b1l, W1r, W2l, b2l, W2r, Wrel, gamma, beta, out):
    fp32, bf16, i32 = mybir.dt.float32, mybir.dt.bfloat16, mybir.dt.int32
    ALU = mybir.AluOpType
    ACT = mybir.ActivationFunctionType
    ds = bass.ds

    tables = [nc.dram_tensor(f"node_table_{n}", [BLOCKS * P, ROW], bf16) for n in range(SAGE)]
    rel_table = nc.dram_tensor("node_relation_table", [BLOCKS * P * RELS, ROW], bf16)

    ctx = ExitStack()
    with ctx:
        def sb(name, shape, dt):
            return ctx.enter_context(nc.sbuf_tensor(name, shape, dt))

        def sem(name):
            return ctx.enter_context(nc.semaphore(name))

        X = sb("X", [P, BLOCKS, D], fp32)
        H = sb("H", [P, BLOCKS, D], fp32)
        G = sb("G", [P, G_SLOTS, ROW], bf16)
        M = sb("M", [P, 2, QUAD, P], bf16)
        rel_dst = sb("rel_dst", [P, VT], fp32)
        node_idx = sb("node_idx", [P, CHUNKS * P], i32)
        rel_idx = sb("rel_idx", [P, CHUNKS * P], i32)
        run_idx = sb("run_idx", [P, 2, G_SLOTS], i32)
        stage = sb("stage", [P, 2, RELS, ROW], bf16)
        rest = sb("rest", [P, RELS, D], fp32)
        ident = sb("ident", [P, P], fp32)
        ones = sb("ones", [P, P], fp32)
        zrow = sb("zrow", [1, 2 * D], bf16)
        node_iota = sb("node_iota", [P, P], bf16)
        eps = sb("eps", [P, 1], fp32)
        ones_col = sb("ones_col", [P, 1], bf16)
        bounds = sb("bounds", [1, BOUNDS], i32)
        rdeg = sb("rdeg", [P, BLOCKS], fp32)
        mean = sb("mean", [P, 2 * D], fp32)
        h_now = sb("h_now", [P, D], fp32)
        x1_now = sb("x1_now", [P, D], fp32)
        turned = sb("turned", [P, 2 * KC, P], fp32)
        x1T = sb("x1T", [P, KC, P], fp32)
        wT = [sb(f"wT{n}", [P, KC, D], fp32) for n in range(4)]
        biases = sb("biases", [1, 2, D], fp32)
        wrel = sb("wrel", [P, KC, RELS * D], fp32)
        stats = sb("stats", [P, GROUP, 6], fp32)
        moments = sb("moments", [P, GROUP, 2], fp32)
        rstd = sb("rstd", [P, GROUP], fp32)
        nbias = sb("nbias", [P, GROUP], fp32)
        gamma_b, beta_b = wT[0][:, 0, :], wT[0][:, 1, :]
        square = rest[:, 0:2, :]
        scale_b = rest[:, 2, :]
        shift = rest[:, 3, :]

        flat = H[:, :, :].rearrange("p b d -> p (b d)")
        taken = [0]

        def scratch(n, dt=fp32):
            at, taken[0] = taken[0], taken[0] + n
            return flat[:, at:at + n].bitcast(dt) if dt != fp32 else flat[:, at:at + n]

        EC = CHUNKS * P
        dst_i, src_i, typ_i = scratch(EC, i32), scratch(EC, i32), scratch(EC, i32)
        dst_f, src_f, typ_f = scratch(EC), scratch(EC), scratch(EC)
        below = scratch(CHUNKS * 64)
        thresholds = scratch(64)
        visit_iota = scratch(VT)
        column_iota = scratch(VT)
        started = scratch(VT)
        tile_of = scratch(VT)
        tile_iota = scratch(CHUNKS)
        part_iota = scratch(1)
        fourth_i = scratch(1, i32)
        fourth = scratch(1)
        first_visit = scratch(1)
        minus_block = scratch(P)
        at_tile = [scratch(VT), scratch(VT)]
        assert taken[0] <= BLOCKS * D

        ring = G[:, :, :].rearrange("p s r -> p (s r)").bitcast(fp32)
        w_in = [ring[:, n * KC * D:(n + 1) * KC * D].rearrange("p (o i) -> p o i", o=KC) for n in range(4)]

        rest_2 = ring[:, 4 * KC * D:4 * KC * D + GROUP * D].rearrange("p (b d) -> p b d", d=D)

        rest_2 = ring[:, 4 * KC * D:4 * KC * D + GROUP * D].rearrange("p (b d) -> p b d", d=D)

        rest_2 = ring[:, 4 * KC * D:4 * KC * D + GROUP * D].rearrange("p (b d) -> p b d", d=D)

        rest_2 = ring[:, 4 * KC * D:4 * KC * D + GROUP * D].rearrange("p (b d) -> p b d", d=D)

        rest_2 = ring[:, 4 * KC * D:4 * KC * D + GROUP * D].rearrange("p (b d) -> p b d", d=D)

        banks = ctx.enter_context(nc.psum_tensor("banks", [P, 8, 512], fp32))
        AGG, TURN, LIN, REL = 0, 2, 3, 4

        pads = sem("pads")
        xpad = sem("xpad")
        made = sem("made")
        edges_in = sem("edges_in")
        consts_in = sem("consts_in")
        norm_in = sem("norm_in")
        weights_in = sem("weights_in")
        x_in = [sem(f"x_in{g}") for g in range(GROUPS)]
        fourth_ready = sem("fourth_ready")
        dst_ready = sem("dst_ready")
        sources_ready = sem("sources_ready")
        below_ready = sem("below_ready")
        sources_turned = sem("sources_turned")
        idx_ready = sem("idx_ready")
        counted = sem("counted")
        first_ready = sem("first_ready")
        bounds_ready = sem("bounds_ready")
        started_ready = sem("started_ready")
        spread = sem("spread")
        tile_of_ready = sem("tile_of_ready")
        at_tile_ready = sem("at_tile_ready")
        rel_summed = sem("rel_summed")
        rel_dst_ready = sem("rel_dst_ready")
        weights_turned = sem("weights_turned")
        weights_ready = sem("weights_ready")
        x_hi = sem("x_hi")
        x_rest = sem("x_rest")
        x_mid = sem("x_mid")
        x_low = sem("x_low")
        x_out = [sem("x_out0"), sem("x_out1")]
        g_in = [sem(f"g_in{k}") for k in range(RUN)]
        run_copied = sem("run_copied")
        quad_free = sem("quad_free")
        m_ready = sem("m_ready")
        m_free = sem("m_free")
        agg_done = sem("agg_done")
        deg_clamped = sem("deg_clamped")
        deg_ready = sem("deg_ready")
        agg_read = sem("agg_read")
        turn_done = sem("turn_done")
        turn_read = sem("turn_read")
        lin_done = sem("lin_done")
        lin_read = sem("lin_read")
        h_rest = sem("h_rest")
        h_mid = sem("h_mid")
        h_split = sem("h_split")
        table_out = sem("table_out")
        y_stats = sem("y_stats")
        y_moments = sem("y_moments")
        y_root = sem("y_root")
        y_rstd = sem("y_rstd")
        x1_ready = sem("x1_ready")
        x1_kept = sem("x1_kept")
        x1_turned = sem("x1_turned")
        x1T_ready = sem("x1T_ready")
        rel_done = sem("rel_done")
        rel_hi = sem("rel_hi")
        rel_read = sem("rel_read")
        rel_mid = sem("rel_mid")
        rel_split = sem("rel_split")
        rel_out = sem("rel_out")
        half_dev = sem("half_dev")
        first_copied = sem("first_copied")
        first_summed = sem("first_summed")
        shift_ready = sem("shift_ready")
        sq_ready = sem("sq_ready")
        sums_done = sem("sums_done")
        bn_step = sem("bn_step")
        bn_root = sem("bn_root")
        scale_ready = sem("scale_ready")
        offset_added = sem("offset_added")
        scaled = sem("scaled")
        z_ready = sem("z_ready")
        z_stats = sem("z_stats")
        z_moments = sem("z_moments")
        z_root = sem("z_root")
        z_rstd = sem("z_rstd")
        norm_ready = sem("norm_ready")
        normed = sem("normed")
        out_done = [sem("out_done0"), sem("out_done1")]

        def wait_apart(eng, semaphore, value):
            if not isinstance(value, int):
                value = eng.to_reg(value)
            eng.wait_ge(made, 1)
            eng.wait_ge(semaphore, value)

        def over_blocks(eng, steps, peel=1):
            deep = max(lag for lag, _ in steps)
            first = deep + peel
            last = first + (BLOCKS - first) // 2 * 2

            def blocks(i, parity, known):
                for lag, step in steps:
                    if not known or 0 <= i - lag < BLOCKS:
                        step(i - lag, (parity - lag) & 1)

            for i in range(first):
                blocks(i, i & 1, True)
            with eng.Fori(first, last - 1, 2) as i:
                blocks(i, first & 1, False)
                blocks(i + 1, (first + 1) & 1, False)
            for i in range(last, BLOCKS + deep):
                blocks(i, i & 1, True)

        def is_first(j):
            return isinstance(j, int) and j == 0

        def ahead(j, k):
            return min(j + k, BLOCKS) if isinstance(j, int) else j + k

        block = ctx.enter_context(nc.Block())

        @block.sync
        def _(sp):
            whole = (CHUNKS - 1) * P * P
            tail = WHOLE_TILES - (CHUNKS - 1) * P
            sp.wait_ge(pads, 3)
            for arr, to in ((src, src_i), (rel, typ_i), (dst, dst_i)):
                to3 = to.rearrange("p (c e) -> p c e", e=P)
                sp.dma_start(to3[:, 0:CHUNKS - 1, :],
                             arr[0:whole].rearrange("(c t e) -> t c e", t=P, e=P)).then_inc(edges_in, 16)
                sp.dma_start(to3[0:tail, CHUNKS - 1, :],
                             arr[whole:whole + tail * P].rearrange("(t e) -> t e", e=P)).then_inc(edges_in, 16)
                sp.dma_start(to3[tail:tail + 1, CHUNKS - 1, 0:LAST_EDGES],
                             arr[whole + tail * P:N_EDGES].rearrange("(t e) -> t e", t=1)).then_inc(edges_in, 16)
            sp.wait_ge(xpad, 1)
            for g in range(GROUPS):
                b0, nb = g * GROUP, GROUP - (g == GROUPS - 1)
                sp.dma_start(X[:, b0:b0 + nb, :], x[b0 * P:(b0 + nb) * P, :].rearrange(
                    "(b p) d -> p b d", p=P)).then_inc(x_in[g], 16)
            sp.dma_start(X[0:LAST_ROWS, BLOCKS - 1, :], x[(BLOCKS - 1) * P:N_NODES, :]).then_inc(x_in[GROUPS - 1], 16)
            for w, to in zip((W1l, W1r, W2l, W2r), w_in):
                sp.dma_start(to, w.rearrange("(o p) i -> p o i", p=P)).then_inc(weights_in, 16)
            for k in range(KC):
                sp.dma_start(wrel[:, k, :].rearrange("p (r o) -> p r o", r=RELS),
                             Wrel[:, k * P:(k + 1) * P, :].rearrange("r p o -> p r o")).then_inc(consts_in, 16)
            sp.dma_start(biases[0:1, 0, :], b1l.rearrange("(a d) -> a d", a=1)).then_inc(consts_in, 16)
            sp.dma_start(biases[0:1, 1, :], b2l.rearrange("(a d) -> a d", a=1)).then_inc(consts_in, 16)

            for g in range(GROUPS):
                sp.wait_ge(x_low, g + 1)
                sp.dma_start(tables[0][g * GROUP * P:(g + 1) * GROUP * P, :].rearrange("(b p) c -> p b c", p=P),
                             stage[:, g % 2, 0:GROUP, :]).then_inc(x_out[g % 2], 16)

            sp.wait_ge(lin_done, BLOCKS)
            for to, v in ((gamma_b, gamma), (beta_b, beta)):
                sp.dma_start(to, v.rearrange("(a d) -> a d", a=1).to_broadcast([P, D])).then_inc(norm_in, 16)

            for g in range(GROUPS):
                b0, nb = g * GROUP, GROUP - (g == GROUPS - 1)
                sp.wait_ge(normed, GROUP * (g + 1))
                sp.dma_start(out[b0 * P:(b0 + nb) * P, :].rearrange("(b p) d -> p b d", p=P),
                             H[:, b0:b0 + nb, :]).then_inc(out_done[g % 2], 16)
            sp.dma_start(out[(BLOCKS - 1) * P:N_NODES, :], H[0:LAST_ROWS, BLOCKS - 1, :]).then_inc(out_done[1], 16)
            sp.wait_ge(out_done[0], 16 * ((GROUPS + 1) // 2))
            sp.wait_ge(out_done[1], 16 * (GROUPS // 2 + 1))

        @block.gpsimd
        def _(pool):
            gp = nc.gpsimd
            for to, v in ((dst_i, FAR), (src_i, 0), (typ_i, 0)):
                gp.memset(to[:, (CHUNKS - 1) * P:], v).then_inc(pads, 1)
            gp.memset(X[:, BLOCKS - 1, :], 0.0).then_inc(xpad, 1)
            gp.memset(ident[:, :], 0.0).then_inc(made, 1)
            gp.memset(ones[:, :], 1.0).then_inc(made, 1)
            pool.wait_ge(made, 1)
            gp.affine_select(out=ident[:, :], in_=ident[:, :], compare_op=ALU.not_equal, fill=1.0, base=0,
                             pattern=[[-1, P]], channel_multiplier=1).then_inc(made, 1)

            def count(to, width, step, base, by_partition):
                gp.iota(to, pattern=[[step, width]], base=base, channel_multiplier=by_partition,
                        allow_small_or_imprecise_dtypes=True).then_inc(made, 1)

            count(thresholds, 64, P, 0, 0)
            gp.iota(visit_iota.rearrange("p (w i) -> p w i", i=QUAD), pattern=[[1, VISITS], [0, QUAD]], base=0,
                    channel_multiplier=0, allow_small_or_imprecise_dtypes=True).then_inc(made, 1)
            count(column_iota, VT, 1, 0, 0)
            count(tile_iota, CHUNKS, P, -QUAD, 1)
            gp.iota(fourth_i, pattern=[[0, 1]], base=0, channel_multiplier=1).then_inc(made, 1)
            count(part_iota, 1, 1, 0, 1)
            count(node_iota[:, :], P, 1, -P, 0)
            gp.memset(minus_block, -float(P)).then_inc(made, 1)
            gp.memset(zrow[:, :], 0.0).then_inc(made, 1)
            gp.memset(ones_col[:, :], 1.0).then_inc(made, 1)
            gp.memset(eps[:, :], EPS).then_inc(made, 1)
            pool.wait_ge(idx_ready, 4)

            for n in range(SAGE + 1):
                idx = node_idx if n < SAGE else rel_idx
                table = tables[n] if n < SAGE else rel_table
                copies = n * RUNS
                freed = n * (QUADS - 1)
                if n == 0:
                    pool.wait_ge(weights_turned, 4)
                    pool.wait_ge(x_out[0], 16 * ((GROUPS + 1) // 2))
                    pool.wait_ge(x_out[1], 16 * (GROUPS // 2))
                elif n < SAGE:
                    pool.wait_ge(table_out, 16 * BLOCKS * n)
                else:
                    pool.wait_ge(rel_out, 16 * BLOCKS)

                def gathers(run, parity, first=False, last=False):
                    pool.wait_ge(run_copied, run + (copies + 1))
                    for s in range(G_SLOTS):
                        k = s // QUAD
                        if s % QUAD == 0 and not first:
                            wait_apart(pool, quad_free, run * RUN + (freed + k + 1 - RUN))
                        if s == G_SLOTS - QUAD and not last:
                            gp.tensor_copy(run_idx[:, 1 - parity, :],
                                           idx[:, ds((run + 1) * G_SLOTS, G_SLOTS)]).then_inc(run_copied, 1)
                        gp.indirect_dma_start(
                            out=G[:, s, :], out_offset=None, in_=table[:, :],
                            in_offset=bass.IndirectOffsetOnAxis(ap=run_idx[:, parity, s:s + 1], axis=0),
                        ).then_inc(g_in[k], 16)

                gp.tensor_copy(run_idx[:, 0, :], idx[:, 0:G_SLOTS]).then_inc(run_copied, 1)
                gathers(0, 0, first=True)
                gathers(1, 1)
                with pool.Fori(2, RUNS - 1, 2) as run:
                    gathers(run, 0)
                    gathers(run + 1, 1)
                gathers(RUNS - 1, 0, last=True)

            pool.wait_ge(scale_ready, 1)
            for g in range(GROUPS):
                part = H[:, g * GROUP:(g + 1) * GROUP, :]
                gp.tensor_tensor(part, part, scale_b.unsqueeze(1).to_broadcast([P, GROUP, D]),
                                 ALU.mult).then_inc(scaled, 1)

        @block.tensor
        def _(pe):
            te = nc.tensor
            pe.wait_ge(made, 14)
            pe.wait_ge(sources_ready, 2)
            for k, (arr, c0, c1) in enumerate(SOURCE_LOTS):
                for c in range(c0, c1):
                    last = te.transpose(banks[:, REL + k, (c - c0) * P:(c - c0 + 1) * P],
                                        (src_f, typ_f)[arr][:, c * P:(c + 1) * P], ident[:, :])
                last.then_inc(sources_turned, 1)
            pe.wait_ge(below_ready, CHUNKS)
            pe.wait_ge(fourth_ready, 2)
            for c in range(CHUNKS):
                te.matmul(banks[0:BOUNDS, AGG, 0:1], below[:, c * 64:c * 64 + BOUNDS], fourth,
                          start=(c == 0), stop=(c == CHUNKS - 1))
            for c in range(CHUNKS):
                last = te.matmul(banks[0:1, AGG + 1, 0:BOUNDS], fourth, below[:, c * 64:c * 64 + BOUNDS],
                                 start=(c == 0), stop=(c == CHUNKS - 1))
            last.then_inc(counted, 1)
            pe.wait_ge(started_ready, 1)
            for h in range(2):
                last = te.matmul(banks[:, TURN + h, 0:HALF], ones[0:BLOCKS, :],
                                 started[0:BLOCKS, h * HALF:(h + 1) * HALF], start=True, stop=True)
            last.then_inc(spread, 1)
            for h in range(2):
                te.matmul(banks[:, AGG + h, 0:HALF], minus_block[0:BLOCKS, :],
                          started[0:BLOCKS, h * HALF:(h + 1) * HALF], start=True, stop=False)
            for c in range(CHUNKS):
                pe.wait_ge(at_tile_ready, c + 1)
                for h in range(2):
                    last = te.matmul(banks[:, AGG + h, 0:HALF], dst_f[:, c * P:(c + 1) * P],
                                     at_tile[c % 2][:, h * HALF:(h + 1) * HALF], start=False, stop=(c == CHUNKS - 1))
                last.then_inc(rel_summed, 1)
            pe.wait_ge(weights_in, 64)
            pe.wait_ge(idx_ready, 4)
            for n in range(4):
                for k in range(KC):
                    for o in range(KC):
                        last = te.transpose(banks[:, REL + n, (k * KC + o) * P:(k * KC + o + 1) * P],
                                            w_in[n][:, o, k * P:(k + 1) * P], ident[:, :])
                last.then_inc(weights_turned, 1)
            pe.wait_ge(weights_ready, 4)
            pe.wait_ge(consts_in, 16 * 4)
            pe.wait_ge(bounds_ready, 1)
            pe.wait_ge(rel_dst_ready, 1)
            for g in range(GROUPS):
                pe.wait_ge(x_in[g], 16 if g < GROUPS - 1 else 32)
            pe.sem_inc(m_free, 1)

            for n in range(SAGE + 1):
                before = n * BLOCKS
                wl, wr = (wT[0], wT[1]) if n == 0 else (wT[2], wT[3])
                bias = biases[0:1, min(n, 1), :]

                def visit(run, k, b, parity):
                    pe.wait_ge(m_ready, run * RUN + b + (k + n * VISITS + 1))
                    pe.wait_ge(g_in[k], run * (16 * QUAD) + 16 * QUAD * (n * RUNS + 1))
                    bank = AGG + (parity + before) % 2
                    for i in range(QUAD):
                        sel = M[:, (k + parity + n * VISITS) % 2, i, :]
                        first = te.matmul(banks[:, bank, :], sel, G[:, k * QUAD + i, 0:2 * D],
                                          start=False, stop=False, skip_group_check=True)
                        if i == 0:
                            first.then_inc(m_free, 1)
                        if n == 0:
                            te.matmul(banks[:, REL + parity, 0:1], sel, ones_col[:, :],
                                      start=False, stop=False, skip_group_check=True)
                        last = te.matmul(banks[:, bank, 0:D], sel, G[:, k * QUAD + i, 2 * D:3 * D],
                                         start=False, stop=False, skip_group_check=True)
                    return last

                def visits(b, parity):
                    if n > 0 or not isinstance(b, int) or b >= 2:
                        pe.wait_ge(agg_read, b + (before - 1))
                    for bank, width in [(AGG + (parity + before) % 2, 2 * D)] + [(REL + parity, 1)] * (n == 0):
                        te.matmul(banks[:, bank, 0:width], zrow[0:1, 0:P], zrow[0:1, 0:width],
                                  start=True, stop=False, skip_group_check=True)
                    lo = te.value_load(bounds[0:1, ds(b, 1)], min_val=0, max_val=QUADS - 1)
                    hi = te.value_load(bounds[0:1, ds(b + 1, 1)], min_val=0, max_val=QUADS - 1)
                    with pe.Fori(lo >> 2, (hi >> 2) + 1) as run:
                        for k in range(RUN):
                            quad = run * RUN + k
                            with te.If((quad - lo) * (hi - 1 - quad) >= 0):
                                visit(run, k, b, parity).then_inc(quad_free, 1)
                            with te.If(quad == hi):
                                visit(run, k, b, parity).then_inc(agg_done, 1)

                def turn(j, parity):
                    pe.wait_ge(agg_read, j + (before + 1))
                    if n == SAGE - 1 and (not isinstance(j, int) or j > 1):
                        pe.wait_ge(x1T_ready, j - 1)
                    if n > 0 or not isinstance(j, int) or j > 0:
                        pe.wait_ge(turn_read, j + before)
                    for k in range(KC):
                        for half in range(2):
                            te.matmul(banks[:, TURN, k * P:(k + 1) * P],
                                      mean[:, half * D + k * P:half * D + (k + 1) * P], ident[:, :],
                                      start=(half == 0), stop=(half == 1))
                    for k in range(KC):
                        last = te.transpose(banks[:, TURN, (KC + k) * P:(KC + k + 1) * P],
                                            h_now[:, k * P:(k + 1) * P], ident[:, :])
                    last.then_inc(turn_done, 1)

                def linear(j, parity):
                    pe.wait_ge(turn_read, j + (before + 1))
                    if n > 0 or not isinstance(j, int) or j > 0:
                        pe.wait_ge(lin_read, j + before)
                    te.matmul(banks[:, LIN, 0:D], ones[0:1, :], bias, start=True, stop=False)
                    for k in range(2 * KC):
                        last = te.matmul(banks[:, LIN, 0:D], turned[:, k, :], (wl, wr)[k // KC][:, k % KC, :],
                                         start=False, stop=(k == 2 * KC - 1))
                    last.then_inc(lin_done, 1)

                def turn_x1(j, parity):
                    pe.wait_ge(x1_ready, j + 1)
                    pe.wait_ge(turn_read, ahead(j, 2) + before)
                    for k in range(KC):
                        last = te.transpose(banks[:, TURN, k * P:(k + 1) * P], x1_now[:, k * P:(k + 1) * P],
                                            ident[:, :])
                    last.then_inc(x1_turned, 1)

                def relations(j, parity):
                    pe.wait_ge(x1T_ready, j + 1)
                    if not is_first(j):
                        pe.wait_ge(rel_read, j)
                    for q in range(4):
                        for k in range(KC):
                            last = te.matmul(banks[:, REL + q, :], x1T[:, k, :], wrel[:, k, q * 512:(q + 1) * 512],
                                             start=(k == 0), stop=(k == KC - 1))
                    last.then_inc(rel_done, 1)

                def sum_first(j, parity):
                    if isinstance(j, int) and j == 0:
                        pe.wait_ge(first_copied, 1)
                        te.matmul(banks[:, TURN, 0:D], ones[:, :], mean[:, 0:D], start=True, stop=False)
                        te.matmul(banks[:, TURN, 0:D], ones[:, :], mean[:, D:2 * D], start=False,
                                  stop=True).then_inc(first_summed, 1)

                def sums(j, parity):
                    rows = LAST_ROWS if isinstance(j, int) and j == BLOCKS - 1 else P
                    pe.wait_ge(agg_read, j + (before + 1))
                    pe.wait_ge(sq_ready, j + 1)
                    te.matmul(banks[:, LIN, 0:D], ones[0:rows, :], H[0:rows, j, :],
                              start=False, stop=False, skip_group_check=True)
                    te.matmul(banks[:, LIN, D:2 * D], ones[0:rows, :], square[0:rows, parity, :],
                              start=False, stop=False, skip_group_check=True).then_inc(sums_done, 1)

                if n < SAGE - 1:
                    over_blocks(pe, [(0, visits), (1, turn), (1, linear)])
                elif n == SAGE - 1:
                    over_blocks(pe, [(0, visits), (3, turn_x1), (3, relations), (1, turn), (1, linear)])
                else:
                    pe.wait_ge(lin_read, SAGE * BLOCKS)
                    te.matmul(banks[:, LIN, 0:2 * D], zrow[0:1, 0:P], zrow[0:1, :],
                              start=True, stop=False, skip_group_check=True)
                    over_blocks(pe, [(0, visits), (1, sum_first), (2, sums)])

        @block.vector
        def _(dve):
            ve = nc.vector
            dve.wait_ge(edges_in, 16 * 9)
            ve.tensor_copy(src_f, src_i).then_inc(sources_ready, 1)
            ve.scalar_tensor_tensor(out=typ_f, in0=src_i, scalar=float(RELS), in1=typ_i,
                                    op0=ALU.mult, op1=ALU.add).then_inc(sources_ready, 1)
            ve.tensor_copy(dst_f, dst_i).then_inc(dst_ready, 1)
            dve.wait_ge(made, 14)
            ve.tensor_scalar(fourth_i, fourth_i, QUAD - 1, None, ALU.bitwise_and).then_inc(fourth_ready, 1)
            dve.wait_ge(fourth_ready, 1)
            ve.tensor_scalar(fourth, fourth_i, float(QUAD - 1), None, ALU.is_equal).then_inc(fourth_ready, 1)
            dve.wait_ge(dst_ready, 1)
            for c in range(CHUNKS):
                ve.tensor_scalar(below[:, c * 64:(c + 1) * 64], thresholds, dst_f[:, (c + 1) * P - 1:(c + 1) * P],
                                 None, ALU.is_gt).then_inc(below_ready, 1)
            for k, (arr, c0, c1) in enumerate(SOURCE_LOTS):
                dve.wait_ge(sources_turned, k + 1)
                ve.tensor_copy((node_idx, rel_idx)[arr][:, c0 * P:c1 * P],
                               banks[:, REL + k, 0:(c1 - c0) * P]).then_inc(idx_ready, 1)

            for g in range(GROUPS):
                part = stage[:, g % 2, 0:GROUP, :]
                left = (rest[:, 0:GROUP, :], rest_2)[g % 2]
                dve.wait_ge(x_hi, g + 1)
                ve.tensor_tensor(left, X[:, g * GROUP:(g + 1) * GROUP, :], part[:, :, 0:D],
                                 ALU.subtract).then_inc(x_rest, 1)
                if g == 0:
                    dve.wait_ge(counted, 1)
                    ve.tensor_tensor(first_visit[0:BOUNDS, :], banks[0:BOUNDS, AGG, 0:1], part_iota[0:BOUNDS, :],
                                     ALU.add).then_inc(first_ready, 1)
                    ve.tensor_copy(bounds[0:1, :], banks[0:1, AGG + 1, 0:BOUNDS]).then_inc(bounds_ready, 1)
                    dve.wait_ge(first_ready, 1)
                    ve.tensor_scalar(started[0:BLOCKS, :], visit_iota[0:BLOCKS, :], first_visit[0:BLOCKS, :],
                                     None, ALU.is_ge).then_inc(started_ready, 1)
                dve.wait_ge(x_mid, g + 1)
                dve.wait_ge(x_rest, g + 1)
                ve.tensor_tensor(part[:, :, 2 * D:3 * D], left, part[:, :, D:2 * D],
                                 ALU.subtract).then_inc(x_low, 1)

            dve.wait_ge(spread, 1)
            for h in range(2):
                ve.scalar_tensor_tensor(out=tile_of[:, h * HALF:(h + 1) * HALF], in0=banks[:, TURN + h, 0:HALF],
                                        scalar=-float(QUAD), in1=column_iota[:, h * HALF:(h + 1) * HALF],
                                        op0=ALU.mult, op1=ALU.add).then_inc(tile_of_ready, 1)
            dve.wait_ge(tile_of_ready, 2)
            for c in range(CHUNKS):
                if c >= 2:
                    dve.wait_ge(rel_summed, c - 1)
                ve.tensor_scalar(at_tile[c % 2], tile_of, tile_iota[:, c:c + 1], None,
                                 ALU.is_equal).then_inc(at_tile_ready, 1)
            dve.wait_ge(rel_summed, CHUNKS)
            for h in range(2):
                last = ve.tensor_copy(rel_dst[:, h * HALF:(h + 1) * HALF], banks[:, AGG + h, 0:HALF])
            last.then_inc(rel_dst_ready, 1)
            dve.wait_ge(rel_dst_ready, 1)
            dve.wait_ge(bounds_ready, 1)

            for n in range(SAGE + 1):
                before = n * BLOCKS

                def selections(b, parity):
                    lo = ve.value_load(bounds[0:1, ds(b, 1)], min_val=0, max_val=QUADS - 1)
                    hi = ve.value_load(bounds[0:1, ds(b + 1, 1)], min_val=0, max_val=QUADS - 1)
                    with dve.Fori(lo, hi + 1) as quad:
                        dve.wait_ge(m_free, quad + b + (n * VISITS + 1))
                        ve.tensor_tensor(
                            M[:, (quad + b + n * VISITS) & 1, :, :],
                            node_iota[:, :].unsqueeze(1).to_broadcast([P, QUAD, P]),
                            rel_dst[:, ds((quad + b) * QUAD, QUAD)].unsqueeze(2).to_broadcast([P, QUAD, P]),
                            ALU.is_equal).then_inc(m_ready, 1)

                def degrees(j, parity):
                    dve.wait_ge(agg_done, j + 1)
                    ve.tensor_scalar(rdeg[:, ds(j, 1)], banks[:, REL + parity, 0:1], 1.0, None,
                                     ALU.max).then_inc(deg_clamped, 1)
                    wait_apart(dve, deg_clamped, j + 1)
                    ve.reciprocal(rdeg[:, ds(j, 1)], rdeg[:, ds(j, 1)]).then_inc(deg_ready, 1)

                def split_h(j, parity):
                    row = stage[:, parity, j & 3, :]
                    dve.wait_ge(lin_read, j + (before + 1))
                    if n > 0 or not isinstance(j, int) or j > 0:
                        dve.wait_ge(h_split, j + before)
                    ve.tensor_tensor(rest[:, 0, :], H[:, j, :], row[:, 0:D], ALU.subtract).then_inc(h_rest, 1)
                    dve.wait_ge(h_rest, j + (before + 1))
                    ve.tensor_copy(row[:, D:2 * D], rest[:, 0, :]).then_inc(h_mid, 1)
                    dve.wait_ge(h_mid, j + (before + 1))
                    ve.tensor_tensor(row[:, 2 * D:3 * D], rest[:, 0, :], row[:, D:2 * D],
                                     ALU.subtract).then_inc(h_split, 1)

                def layernorm(j, parity):
                    dve.wait_ge(lin_done, j + (before + 1))
                    if not isinstance(j, int) or j > 0:
                        dve.wait_ge(x1_turned, j)
                        dve.wait_ge(x1_kept, j)
                    ve.tensor_tensor(x1_now[:, :], banks[:, LIN, 0:D], X[:, j, :], ALU.add).then_inc(lin_read, 1)
                    dve.wait_ge(lin_read, j + (before + 1))
                    ve.bn_stats(stats[:, 0, :], x1_now[:, :]).then_inc(y_stats, 1)
                    wait_apart(dve, y_stats, j + 1)
                    ve.bn_aggr(moments[:, 0, :], stats[:, 0, :]).then_inc(y_moments, 1)
                    dve.wait_ge(y_root, j + 1)
                    ve.reciprocal(rstd[:, 0:1], rstd[:, 0:1]).then_inc(y_rstd, 1)
                    dve.wait_ge(y_rstd, j + 1)
                    ve.tensor_scalar(x1_now[:, :], x1_now[:, :], moments[:, 0, 0:1], rstd[:, 0:1], ALU.subtract,
                                     ALU.mult).then_inc(x1_ready, 1)

                def split_relations(j, parity):
                    part = stage[:, parity, :, :]
                    values = banks[:, REL:REL + 4, :].rearrange("p q (r d) -> p (q r) d", r=2)
                    dve.wait_ge(rel_hi, j + 1)
                    if not isinstance(j, int) or j > 0:
                        dve.wait_ge(rel_split, j)
                    ve.tensor_tensor(rest[:, :, :], values, part[:, :, 0:D], ALU.subtract).then_inc(rel_read, 1)
                    dve.wait_ge(rel_read, j + 1)
                    ve.tensor_copy(part[:, :, D:2 * D], rest[:, :, :]).then_inc(rel_mid, 1)
                    dve.wait_ge(rel_mid, j + 1)
                    ve.tensor_tensor(part[:, :, 2 * D:3 * D], rest[:, :, :], part[:, :, D:2 * D],
                                     ALU.subtract).then_inc(rel_split, 1)

                def deviations(j, parity):
                    bank = AGG + (parity + before) % 2
                    dve.wait_ge(agg_done, j + (before + 1))
                    if isinstance(j, int) and j == 0:
                        ve.tensor_copy(mean[:, :], banks[:, bank, :]).then_inc(first_copied, 1)
                        dve.wait_ge(first_summed, 1)
                        ve.tensor_scalar(shift, banks[:, TURN, 0:D], 1.0 / P, None, ALU.mult).then_inc(shift_ready, 1)
                        dve.wait_ge(shift_ready, 1)
                    ve.tensor_tensor(H[:, j, :], banks[:, bank, 0:D], shift, ALU.subtract).then_inc(half_dev, 1)
                    dve.wait_ge(half_dev, j + 1)
                    ve.tensor_tensor(H[:, j, :], banks[:, bank, D:2 * D], H[:, j, :], ALU.add).then_inc(agg_read, 1)

                if n == 0:
                    over_blocks(dve, [(0, selections), (1, degrees), (2, split_h)])
                elif n < SAGE - 1:
                    over_blocks(dve, [(0, selections), (2, split_h)])
                elif n == SAGE - 1:
                    over_blocks(dve, [(0, selections), (2, layernorm), (4, split_relations)])
                else:
                    over_blocks(dve, [(0, selections), (1, deviations)])

            steps = [0]

            def then(ins):
                steps[0] += 1
                ins.then_inc(bn_step, 1)
                dve.wait_ge(bn_step, steps[0])

            dve.wait_ge(norm_in, 32)
            dve.wait_ge(sums_done, BLOCKS)
            then(ve.tensor_scalar(mean[:, 0:D], banks[:, LIN, 0:D], 1.0 / N_NODES, None, ALU.mult))
            then(ve.tensor_tensor(shift, mean[:, 0:D], mean[:, 0:D], ALU.mult))
            then(ve.scalar_tensor_tensor(out=scale_b, in0=banks[:, LIN, D:2 * D], scalar=1.0 / N_NODES,
                                         in1=shift, op0=ALU.mult, op1=ALU.subtract))
            dve.wait_ge(bn_root, 1)
            then(ve.reciprocal(scale_b, scale_b))
            then(ve.tensor_tensor(scale_b, scale_b, gamma_b, ALU.mult))
            ve.tensor_tensor(mean[:, 0:D], mean[:, 0:D], scale_b, ALU.mult).then_inc(scale_ready, 1)
            dve.wait_ge(scale_ready, 1)
            then(ve.tensor_tensor(shift, beta_b, mean[:, 0:D], ALU.subtract))
            for g in range(GROUPS):
                b0 = g * GROUP
                xg, zg = X[:, b0:b0 + GROUP, :], H[:, b0:b0 + GROUP, :]
                ve.tensor_tensor(xg, xg, shift.unsqueeze(1).to_broadcast([P, GROUP, D]),
                                 ALU.add).then_inc(offset_added, 1)
                dve.wait_ge(offset_added, g + 1)
                dve.wait_ge(scaled, g + 1)
                ve.tensor_tensor(zg, zg, xg, ALU.add).then_inc(z_ready, 1)
                dve.wait_ge(z_ready, g + 1)
                if g > 0:
                    dve.wait_ge(normed, b0)
                for i in range(GROUP):
                    ve.bn_stats(stats[:, i, :], H[:, b0 + i, :]).then_inc(z_stats, 1)
                dve.wait_ge(z_stats, b0 + GROUP)
                for i in range(GROUP):
                    ve.bn_aggr(moments[:, i, :], stats[:, i, :]).then_inc(z_moments, 1)
                dve.wait_ge(z_root, g + 1)
                ve.reciprocal(rstd[:, :], rstd[:, :]).then_inc(z_rstd, 1)
                dve.wait_ge(z_rstd, g + 1)
                ve.scalar_tensor_tensor(out=nbias[:, :], in0=moments[:, :, 0], scalar=-1.0, in1=rstd[:, :],
                                        op0=ALU.mult, op1=ALU.mult).then_inc(norm_ready, 1)

        @block.scalar
        def _(act):
            sc = nc.scalar
            def x_first(g):
                act.wait_ge(x_in[g], 16 if g < GROUPS - 1 else 32)
                if g >= 2:
                    act.wait_ge(x_out[g % 2], 16 * (g // 2))
                sc.activation(stage[:, g % 2, 0:GROUP, 0:D], X[:, g * GROUP:(g + 1) * GROUP, :],
                              ACT.Copy).then_inc(x_hi, 1)

            x_first(0)
            for g in range(GROUPS):
                if g + 1 < GROUPS:
                    x_first(g + 1)
                act.wait_ge(x_rest, g + 1)
                sc.activation(stage[:, g % 2, 0:GROUP, D:2 * D], (rest[:, 0:GROUP, :], rest_2)[g % 2],
                              ACT.Copy).then_inc(x_mid, 1)
            for n in range(4):
                act.wait_ge(weights_turned, n + 1)
                sc.activation(wT[n][:, :, :], banks[:, REL + n, :].rearrange("p (k o) -> p k o", k=KC),
                              ACT.Copy).then_inc(weights_ready, 1)
            act.wait_ge(x_out[0], 16 * ((GROUPS + 1) // 2))
            act.wait_ge(x_out[1], 16 * (GROUPS // 2))

            for n in range(SAGE + 1):
                before = n * BLOCKS

                def means(j, parity):
                    act.wait_ge(agg_done, j + (before + 1))
                    if n == 0:
                        act.wait_ge(deg_ready, j + 1)
                    if n > 0 or not isinstance(j, int) or j > 0:
                        act.wait_ge(turn_done, j + before)
                    sc.activation(h_now[:, :], (X if n == 0 else H)[:, j, :], ACT.Copy)
                    sc.activation(mean[:, :], banks[:, AGG + (parity + before) % 2, :], ACT.Copy,
                                  scale=rdeg[:, ds(j, 1)]).then_inc(agg_read, 1)

                def take_turned(j, parity):
                    act.wait_ge(turn_done, j + (before + 1))
                    if n > 0 or not isinstance(j, int) or j > 0:
                        act.wait_ge(lin_done, j + before)
                    sc.activation(turned[:, :, :], banks[:, TURN, :].rearrange("p (k m) -> p k m", m=P),
                                  ACT.Copy).then_inc(turn_read, 1)

                def hidden(j, parity):
                    wait_apart(act, lin_done, j + (before + 1))
                    sc.activation(H[:, j, :], banks[:, LIN, 0:D], ACT.Relu)
                    sc.activation(stage[:, parity, j & 3, 0:D], banks[:, LIN, 0:D], ACT.Relu).then_inc(lin_read, 1)

                def write_h(j, parity):
                    act.wait_ge(h_split, j + (before + 1))
                    if n > 0 or not isinstance(j, int) or j > 0:
                        act.wait_ge(table_out, (j + before) * 16)
                    act.dma_start(tables[n + 1][ds(j * P, P), :], stage[:, parity, j & 3, :]).then_inc(table_out, 16)

                def root(j, parity):
                    act.wait_ge(y_moments, j + 1)
                    if not isinstance(j, int) or j > 0:
                        act.wait_ge(x1_ready, j)
                    sc.activation(rstd[:, 0:1], moments[:, 0, 1:2], ACT.Sqrt, bias=eps[:, :]).then_inc(y_root, 1)

                def keep_x1(j, parity):
                    act.wait_ge(x1_ready, j + 1)
                    sc.activation(X[:, j, :], x1_now[:, :], ACT.Copy).then_inc(x1_kept, 1)

                def take_x1T(j, parity):
                    act.wait_ge(x1_turned, j + 1)
                    if not isinstance(j, int) or j > 0:
                        act.wait_ge(rel_done, j)
                    sc.activation(x1T[:, :, :], banks[:, TURN, 0:D].rearrange("p (k m) -> p k m", m=P),
                                  ACT.Copy).then_inc(x1T_ready, 1)

                def first_part(j, parity):
                    if not isinstance(j, int) or j >= 2:
                        act.wait_ge(rel_out, (j - 1) * 16)
                    act.wait_ge(rel_done, j + 1)
                    sc.activation(stage[:, parity, :, 0:D],
                                  banks[:, REL:REL + 4, :].rearrange("p q (r d) -> p (q r) d", r=2),
                                  ACT.Copy).then_inc(rel_hi, 1)

                def write_relations(j, parity):
                    act.wait_ge(rel_split, j + 1)
                    act.dma_start(rel_table[ds(j * P * RELS, P * RELS), :].rearrange("(p r) c -> p (r c)", r=RELS),
                                  stage[:, parity, :, :].rearrange("p r c -> p (r c)")).then_inc(rel_out, 16)

                def squares(j, parity):
                    act.wait_ge(agg_read, j + (before + 1))
                    if not isinstance(j, int) or j >= 2:
                        act.wait_ge(sums_done, j - 1)
                    sc.activation(square[:, parity, :], H[:, j, :], ACT.Square).then_inc(sq_ready, 1)

                if n < SAGE - 1:
                    over_blocks(act, [(1, means), (3, write_h), (1, take_turned), (1, hidden)])
                elif n == SAGE - 1:
                    act.wait_ge(table_out, 16 * BLOCKS * (SAGE - 1))
                    over_blocks(act, [(4, first_part), (1, means), (5, write_relations), (3, take_x1T),
                                      (2, root), (2, keep_x1), (1, take_turned)])
                else:
                    over_blocks(act, [(2, squares)], peel=2)

            act.wait_ge(bn_step, 3)
            sc.activation(scale_b, scale_b, ACT.Sqrt, bias=eps[:, :]).then_inc(bn_root, 1)
            for g in range(GROUPS):
                act.wait_ge(z_moments, (g + 1) * GROUP)
                sc.activation(rstd[:, :], moments[:, :, 1], ACT.Sqrt, bias=eps[:, :]).then_inc(z_root, 1)
                act.wait_ge(norm_ready, g + 1)
                for i in range(GROUP):
                    zb = H[:, g * GROUP + i, :]
                    sc.activation(zb, zb, ACT.Identity, scale=rstd[:, i:i + 1],
                                  bias=nbias[:, i:i + 1]).then_inc(normed, 1)


_INS = ['x', 'src', 'dst', 'edge_type_8', 'L0_gnn_W1l', 'L0_gnn_b1l', 'L0_gnn_W1r', 'L0_gnn_W2l', 'L0_gnn_b2l',
        'L0_gnn_W2r', 'L1_gnn_weight', 'L1_gnn_gamma', 'L1_gnn_beta']
_OUT = ((N_NODES, D), 'float32')


def kernel(**inputs):
    import concourse.bacc as _bacc
    from concourse.bass_utils import run_bass_kernel_spmd as _run

    nc = _bacc.Bacc("TRN2", target_bir_lowering=False, num_devices=1)
    arrays, args = {}, []
    for name in _INS:
        a = np.ascontiguousarray(inputs[name])
        arrays[f"in_{name}"] = a
        args.append(nc.dram_tensor(f"in_{name}", a.shape, mybir.dt.from_np(a.dtype), kind="ExternalInput").ap())
    args.append(nc.dram_tensor("result", _OUT[0], mybir.dt.from_np(np.dtype(_OUT[1])), kind="ExternalOutput").ap())
    build_gnn(nc, *args)
    return _run(nc, [arrays], core_ids=[0]).results[0]["result"]
```

```python
import numpy as np
import concourse.bass as bass
from concourse import mybir
from contextlib import ExitStack

P = 128
N_NODES = 6250
D = 256
N_EDGES = 100000
RELS = 8
EPS = 1e-5

BLOCKS = -(-N_NODES // P)
LAST_ROWS = N_NODES - (BLOCKS - 1) * P
WHOLE_TILES = N_EDGES // P
LAST_EDGES = N_EDGES - WHOLE_TILES * P
QUAD = 4
RUN = 4
RUN_TILES = QUAD * RUN
RING = 2 * RUN
G_SLOTS = QUAD * RING
RUNS = -(-N_EDGES // (P * RUN_TILES))
RING_SHIFT = RING.bit_length() - 1
FILLS = (RUNS // 2 + 1, RUNS // 2)
QUADS = RUNS * RUN
TILES = QUADS * QUAD
VISITS = QUADS + BLOCKS - 1
CHUNKS = -(-TILES // P)
BOUNDS = BLOCKS + 1
KC = D // P
GROUP = 7
GROUPS = BLOCKS // GROUP
BY_TENSOR = (2, 3)
BY_POOL = tuple(range(4, GROUPS))
FAR = 1 << 16
M_SLOTS = 4
CONSTANTS = 14
SAGE = 3
G_WIDTH = D + 16
VT = VISITS * QUAD
HALF = VT // 2
HALF_RELS = RELS // 2
SOURCE_LOTS = ((0, 4), (4, CHUNKS))
assert GROUPS * GROUP == BLOCKS and RUNS % 2 == 1 and HALF <= 512 and QUADS * QUAD * P > N_EDGES


def chunk_columns(c, h=None):
    first, end = c * P, min(VT, (c + 1) * P + (BLOCKS - 1) * QUAD)
    return (first, end) if h is None else (max(first, h * HALF), min(end, (h + 1) * HALF))


def build_gnn(nc, x, src, dst, rel, W1l, b1l, W1r, W2l, b2l, W2r, Wrel, gamma, beta, out):
    fp32, bf16, i32 = mybir.dt.float32, mybir.dt.bfloat16, mybir.dt.int32
    ALU = mybir.AluOpType
    ACT = mybir.ActivationFunctionType
    ds = bass.ds

    tables = [x] + [nc.dram_tensor(f"node_table_{n}", [BLOCKS * P, D], fp32) for n in range(1, SAGE)]
    rel_table = nc.dram_tensor("node_relation_table", [BLOCKS * P * RELS, D], fp32)

    ctx = ExitStack()
    with ctx:
        def sb(name, shape, dt):
            return ctx.enter_context(nc.sbuf_tensor(name, shape, dt))

        def sem(name):
            return ctx.enter_context(nc.semaphore(name))

        X = sb("X", [P, BLOCKS, D], fp32)
        H = sb("H", [P, BLOCKS, D], fp32)
        G = sb("G", [P, G_SLOTS, G_WIDTH], fp32)
        M = sb("M", [P, M_SLOTS, QUAD, P], fp32)
        rel_dst = sb("rel_dst", [P, VT], fp32)
        node_idx = sb("node_idx", [P, CHUNKS * P], i32)
        rel_idx = sb("rel_idx", [P, CHUNKS * P], i32)
        run_idx = sb("run_idx", [P, 2, RUN_TILES], i32)
        stage = sb("stage", [P, 2, RELS * D], fp32)
        ident = sb("ident", [P, P], fp32)
        ones = sb("ones", [P, P], fp32)
        zrow = sb("zrow", [1, 2 * D], bf16)
        node_iota = sb("node_iota", [P, P], bf16)
        eps = sb("eps", [P, 1], fp32)
        bounds = sb("bounds", [1, BOUNDS], i32)
        rdeg = sb("rdeg", [P, BLOCKS], fp32)
        mean = sb("mean", [P, D], fp32)
        h_now = sb("h_now", [P, D], fp32)
        x1_now = sb("x1_now", [P, D], fp32)
        turned = sb("turned", [P, 2 * KC, P], fp32)
        x1T = sb("x1T", [P, KC, P], fp32)
        h_next, hT = x1_now, x1T
        wT = [sb(f"wT{n}", [P, KC, D], fp32) for n in range(4)]
        biases = sb("biases", [1, 2, D], fp32)
        wrel = sb("wrel", [P, KC, RELS * D], fp32)
        stats = sb("stats", [P, GROUP, 6], fp32)
        moments = sb("moments", [P, GROUP, 2], fp32)
        rstd = sb("rstd", [P, 2, GROUP], fp32)
        nbias = sb("nbias", [P, 2, GROUP], fp32)
        gamma_b, beta_b = sb("gamma_b", [P, D], fp32)[:, :], sb("beta_b", [P, D], fp32)[:, :]
        scale_b, shift = sb("scale_b", [P, D], fp32)[:, :], sb("shift", [P, D], fp32)[:, :]
        square = turned[:, :, :].rearrange("p (s k) m -> p s (k m)", s=2)

        flat = H[:, :, :].rearrange("p b d -> p (b d)")
        taken = [0]

        def scratch(n, dt=fp32):
            at, taken[0] = taken[0], taken[0] + (-(-n // 2) if dt == bf16 else n)
            return flat[:, at:taken[0]] if dt == fp32 else flat[:, at:taken[0]].bitcast(dt)

        EC = CHUNKS * P
        dst_i, src_i, typ_i = scratch(EC, i32), scratch(EC, i32), scratch(EC, i32)
        dst_f, src_f, typ_f = scratch(EC), scratch(EC), scratch(EC)
        dst_low_i = scratch(EC, i32)
        dst_high, dst_low = scratch(EC, bf16), scratch(EC, bf16)
        below = scratch(CHUNKS * 64, bf16)
        thresholds = scratch(64)
        visit_iota = scratch(VT)
        column_iota = scratch(VT)
        started = scratch(VT, bf16)
        tile_of = scratch(VT)
        tile_iota = scratch(CHUNKS)
        part_iota = scratch(1)
        fourth_i = scratch(1, i32)
        fourth = scratch(2, bf16)[:, 0:1]
        first_visit = scratch(1)
        minus_block = scratch(P, bf16)
        ones_b = scratch(P, bf16)
        at_tile = [scratch(VT, bf16), scratch(VT, bf16)]
        assert taken[0] <= BLOCKS * D

        w_flat = stage[:, :, :].rearrange("p s r -> p (s r)")
        w_in = [w_flat[:, n * KC * D:(n + 1) * KC * D].rearrange("p (o i) -> p o i", o=KC) for n in range(4)]

        banks = ctx.enter_context(nc.psum_tensor("banks", [P, 8, 512], fp32))
        AGG, TURN, LIN, REL = 0, 2, 3, 4

        pads = sem("pads")
        xpad = sem("xpad")
        ident_ready = sem("ident_ready")
        made = sem("made")
        src_in = sem("src_in")
        dst_in = sem("dst_in")
        typ_in = sem("typ_in")
        biases_in = sem("biases_in")
        wrel_in = sem("wrel_in")
        norm_in = sem("norm_in")
        weights_in = sem("weights_in")
        x_in = [sem(f"x_in{g}") for g in range(GROUPS)]
        fourth_ready = sem("fourth_ready")
        dst_ready = sem("dst_ready")
        low_ready = sem("low_ready")
        split_ready = sem("split_ready")
        src_ready = sem("src_ready")
        typ_ready = sem("typ_ready")
        below_ready = sem("below_ready")
        src_turned = sem("src_turned")
        typ_turned = sem("typ_turned")
        node_idx_ready = sem("node_idx_ready")
        rel_idx_ready = sem("rel_idx_ready")
        counted = sem("counted")
        first_ready = sem("first_ready")
        bounds_ready = sem("bounds_ready")
        started_ready = sem("started_ready")
        spread = sem("spread")
        tile_of_ready = sem("tile_of_ready")
        at_tile_ready = sem("at_tile_ready")
        rel_summed = sem("rel_summed")
        rel_dst_ready = sem("rel_dst_ready")
        weights_turned = sem("weights_turned")
        weights_ready = sem("weights_ready")
        g_in = [sem(f"g_in{k}") for k in range(RING)]
        run_copied = [sem("run_copied0"), sem("run_copied1")]
        quad_free = sem("quad_free")
        m_ready = sem("m_ready")
        m_free = sem("m_free")
        agg_done = sem("agg_done")
        deg_clamped = sem("deg_clamped")
        deg_ready = sem("deg_ready")
        agg_read = sem("agg_read")
        turn_done = sem("turn_done")
        turn_read = sem("turn_read")
        lin_done = sem("lin_done")
        lin_read = sem("lin_read")
        hT_done = sem("hT_done")
        hT_ready = sem("hT_ready")
        projected = sem("projected")
        left_taken = sem("left_taken")
        root_kept = sem("root_kept")
        table_out = [sem("table_out0"), sem("table_out1")]
        y_stats = sem("y_stats")
        y_moments = sem("y_moments")
        y_root = sem("y_root")
        y_rstd = sem("y_rstd")
        x1_ready = sem("x1_ready")
        x1_kept = sem("x1_kept")
        x1_turned = sem("x1_turned")
        x1T_ready = sem("x1T_ready")
        rel_done = sem("rel_done")
        low_taken = sem("low_taken")
        high_taken = sem("high_taken")
        rel_out = [sem("rel_out0"), sem("rel_out1")]
        first_copied = sem("first_copied")
        first_summed = sem("first_summed")
        shift_ready = sem("shift_ready")
        sq_ready = sem("sq_ready")
        sums_done = sem("sums_done")
        bn_step = sem("bn_step")
        bn_root = sem("bn_root")
        scale_ready = sem("scale_ready")
        offset_ready = sem("offset_ready")
        offset_added = sem("offset_added")
        offset_in_banks = sem("offset_in_banks")
        offset_by_pool = sem("offset_by_pool")
        first_scaled = sem("first_scaled")
        scaled = sem("scaled")
        z_ready = sem("z_ready")
        z_stats = sem("z_stats")
        z_moments = sem("z_moments")
        z_root = sem("z_root")
        z_rstd = sem("z_rstd")
        norm_ready = sem("norm_ready")
        normed = sem("normed")
        out_done = [sem("out_done0"), sem("out_done1")]

        def wait_apart(eng, semaphore, value):
            if not isinstance(value, int):
                value = eng.to_reg(value)
            eng.wait_ge(made, 1)
            eng.wait_ge(semaphore, value)

        def over_blocks(eng, steps, peel=1, unroll=2):
            deep = max(lag for lag, _ in steps)
            first = deep + peel
            last = first + (BLOCKS - first) // unroll * unroll

            def blocks(i, place, known):
                for lag, step in steps:
                    if not known or 0 <= i - lag < BLOCKS:
                        step(i - lag, (place - lag) % unroll)

            for i in range(first):
                blocks(i, i, True)
            with eng.Fori(first, last - unroll + 1, unroll) as i:
                for place in range(unroll):
                    blocks(i + place if place else i, first + place, False)
            for i in range(last, BLOCKS + deep):
                blocks(i, i, True)

        def is_first(j):
            return isinstance(j, int) and j == 0

        block = ctx.enter_context(nc.Block())

        @block.sync
        def _(sp):
            whole = (CHUNKS - 1) * P * P
            tail = WHOLE_TILES - (CHUNKS - 1) * P

            def load_edges(arr, to, loaded):
                to3 = to.rearrange("p (c e) -> p c e", e=P)
                sp.dma_start(to3[:, 0:CHUNKS - 1, :],
                             arr[0:whole].rearrange("(c t e) -> t c e", t=P, e=P)).then_inc(loaded, 16)
                sp.dma_start(to3[0:tail, CHUNKS - 1, :],
                             arr[whole:whole + tail * P].rearrange("(t e) -> t e", e=P)).then_inc(loaded, 16)
                sp.dma_start(to3[tail:tail + 1, CHUNKS - 1, 0:LAST_EDGES],
                             arr[whole + tail * P:N_EDGES].rearrange("(t e) -> t e", t=1)).then_inc(loaded, 16)

            def load_x(g):
                b0, nb = g * GROUP, GROUP - (g == GROUPS - 1)
                sp.dma_start(X[:, b0:b0 + nb, :], x[b0 * P:(b0 + nb) * P, :].rearrange(
                    "(b p) d -> p b d", p=P)).then_inc(x_in[g], 16)
                if g == GROUPS - 1:
                    sp.wait_ge(xpad, 1)
                    sp.dma_start(X[0:LAST_ROWS, BLOCKS - 1, :], x[(BLOCKS - 1) * P:N_NODES, :]).then_inc(x_in[g], 16)

            def load_first():
                load_edges(rel, typ_i, typ_in)
                load_x(0)
                for w, to in zip((W1l, W1r, W2l, W2r), w_in):
                    sp.dma_start(to, w.rearrange("(o p) i -> p o i", p=P)).then_inc(weights_in, 16)
                for k, b in enumerate((b1l, b2l)):
                    sp.dma_start(biases[0:1, k, :], b.rearrange("(a d) -> a d", a=1)).then_inc(biases_in, 16)

            def load_wrel(k):
                sp.dma_start(wrel[:, k, :].rearrange("p (r o) -> p r o", r=RELS),
                             Wrel[:, k * P:(k + 1) * P, :].rearrange("r p o -> p r o")).then_inc(wrel_in, 16)

            def load_norm():
                for to, v in ((gamma_b, gamma), (beta_b, beta)):
                    sp.dma_start(to, v.rearrange("(a d) -> a d", a=1).to_broadcast([P, D])).then_inc(norm_in, 16)

            sp.wait_ge(pads, 3)
            load_edges(src, src_i, src_in)
            load_edges(dst, dst_i, dst_in)

            later = {1: [load_first]}
            for g in range(1, GROUPS):
                later.setdefault(2 + (g - 1) // 2, []).append(lambda g=g: load_x(g))
            for k in range(KC):
                later[2 + GROUPS // 2 + k] = [lambda k=k: load_wrel(k)]
            later[2 + GROUPS // 2 + KC] = [load_norm]
            for n in range(SAGE + 1):
                idx = node_idx if n < SAGE else rel_idx

                def copy_run(run, parity):
                    half = (parity + n) % 2
                    for k in range(RUN):
                        if not isinstance(run, int) or run >= 2:
                            sp.wait_ge(g_in[parity * RUN + k],
                                       (run - parity) * (8 * QUAD) + 16 * QUAD * n * FILLS[parity])
                        elif n > 0:
                            sp.wait_ge(g_in[(1 - parity) * RUN + k], 16 * QUAD * n * FILLS[1 - parity])
                    sp.dma_start(run_idx[:, half, :], idx[:, ds(run * RUN_TILES, RUN_TILES)]
                                 ).then_inc(run_copied[half], 16)

                sp.wait_ge(node_idx_ready if n < SAGE else rel_idx_ready, len(SOURCE_LOTS))
                peeled = (max(later) // 2 + 1) * 2 if n == 0 else 2
                for run in range(peeled):
                    copy_run(run, run % 2)
                    if n == 0:
                        for load in later.get(run, []):
                            load()
                with sp.Fori(peeled, RUNS - 2, 2) as run:
                    copy_run(run, 0)
                    copy_run(run + 1, 1)
                copy_run(RUNS - 1, 0)

            for g in range(GROUPS):
                b0, nb = g * GROUP, GROUP - (g == GROUPS - 1)
                sp.wait_ge(normed, GROUP * (g + 1))
                sp.dma_start(out[b0 * P:(b0 + nb) * P, :].rearrange("(b p) d -> p b d", p=P),
                             H[:, b0:b0 + nb, :]).then_inc(out_done[g % 2], 16)
            sp.dma_start(out[(BLOCKS - 1) * P:N_NODES, :], H[0:LAST_ROWS, BLOCKS - 1, :]).then_inc(out_done[1], 16)
            sp.wait_ge(out_done[0], 16 * ((GROUPS + 1) // 2))
            sp.wait_ge(out_done[1], 16 * (GROUPS // 2 + 1))

        @block.gpsimd
        def _(pool):
            gp = nc.gpsimd
            for to, v in ((dst_i, FAR), (src_i, 0), (typ_i, 0)):
                gp.memset(to[:, (CHUNKS - 1) * P:], v).then_inc(pads, 1)
            gp.memset(X[:, BLOCKS - 1, :], 0.0).then_inc(xpad, 1)
            gp.memset(ident[:, :], 0.0).then_inc(made, 1)
            pool.wait_ge(made, 1)
            gp.affine_select(out=ident[:, :], in_=ident[:, :], compare_op=ALU.not_equal, fill=1.0, base=0,
                             pattern=[[-1, P]], channel_multiplier=1).then_inc(ident_ready, 1)

            def count(to, width, step, base, by_partition):
                gp.iota(to, pattern=[[step, width]], base=base, channel_multiplier=by_partition,
                        allow_small_or_imprecise_dtypes=True).then_inc(made, 1)

            count(thresholds, 64, P, 0, 0)
            gp.iota(fourth_i, pattern=[[0, 1]], base=0, channel_multiplier=1).then_inc(made, 1)
            count(part_iota, 1, 1, 0, 1)
            gp.iota(visit_iota.rearrange("p (w i) -> p w i", i=QUAD), pattern=[[1, VISITS], [0, QUAD]], base=0,
                    channel_multiplier=0, allow_small_or_imprecise_dtypes=True).then_inc(made, 1)
            gp.memset(minus_block, -float(P)).then_inc(made, 1)
            gp.memset(ones_b, 1.0).then_inc(made, 1)
            count(tile_iota, CHUNKS, P, -QUAD, 1)
            count(column_iota, VT, 1, 0, 0)
            count(node_iota[:, :], P, 1, -P, 0)
            gp.memset(ones[:, :], 1.0).then_inc(made, 1)
            gp.memset(zrow[:, :], 0.0).then_inc(made, 1)
            gp.memset(G[:, :, D:D + 1], 1.0).then_inc(made, 1)
            gp.memset(eps[:, :], EPS).then_inc(made, 1)

            for n in range(SAGE + 1):
                idx = node_idx if n < SAGE else rel_idx
                table = tables[n] if n < SAGE else rel_table
                freed = n * (QUADS - 1)
                if 0 < n < SAGE:
                    for parity in range(2):
                        pool.wait_ge(table_out[parity], 16 * n * ((BLOCKS + 1 - parity) // 2))
                elif n == SAGE:
                    for parity in range(2):
                        pool.wait_ge(rel_out[parity], 16 * ((BLOCKS + 1 - parity) // 2))

                def gathers(run, parity, first=False):
                    half = (parity + n) % 2
                    wait_apart(pool, run_copied[half], run * 8 + 8 * (n * RUNS - half + 2))
                    for s in range(RUN_TILES):
                        k = parity * RUN + s // QUAD
                        if s % QUAD == 0 and not first:
                            wait_apart(pool, quad_free, run * RUN + (freed + s // QUAD + 1 - RING))
                        gp.indirect_dma_start(
                            out=G[:, parity * RUN_TILES + s, 0:D], out_offset=None, in_=table[:, :],
                            in_offset=bass.IndirectOffsetOnAxis(ap=run_idx[:, half, s:s + 1], axis=0),
                        ).then_inc(g_in[k], 16)

                gathers(0, 0, first=True)
                gathers(1, 1, first=True)
                with pool.Fori(2, RUNS - 2, 2) as run:
                    gathers(run, 0)
                    gathers(run + 1, 1)
                gathers(RUNS - 1, 0)

            pool.wait_ge(scale_ready, 1)
            for g in range(1, GROUPS):
                part = H[:, g * GROUP:(g + 1) * GROUP, :]
                gp.tensor_tensor(part, part, scale_b.unsqueeze(1).to_broadcast([P, GROUP, D]),
                                 ALU.mult).then_inc(scaled, 1)
            pool.wait_ge(offset_ready, 1)
            for g in BY_POOL:
                part = X[:, g * GROUP:(g + 1) * GROUP, :]
                gp.tensor_tensor(part, part, shift.unsqueeze(1).to_broadcast([P, GROUP, D]),
                                 ALU.add).then_inc(offset_by_pool, 1)

        @block.tensor
        def _(pe):
            te = nc.tensor
            pe.wait_ge(ident_ready, 1)
            def turn_sources(arr, ready, turned_):
                pe.wait_ge(ready, 1)
                for k, (c0, c1) in enumerate(SOURCE_LOTS):
                    for c in range(c0, c1):
                        last = te.transpose(banks[:, REL + k, (c - c0) * P:(c - c0 + 1) * P],
                                            arr[:, c * P:(c + 1) * P], ident[:, :])
                    last.then_inc(turned_, 1)

            turn_sources(src_f, src_ready, src_turned)
            pe.wait_ge(below_ready, CHUNKS)
            pe.wait_ge(fourth_ready, 2)
            for c in range(CHUNKS):
                te.matmul(banks[0:BOUNDS, AGG, 0:1], below[:, c * 64:c * 64 + BOUNDS], fourth,
                          start=(c == 0), stop=(c == CHUNKS - 1))
            for c in range(CHUNKS):
                last = te.matmul(banks[0:1, AGG + 1, 0:BOUNDS], fourth, below[:, c * 64:c * 64 + BOUNDS],
                                 start=(c == 0), stop=(c == CHUNKS - 1))
            last.then_inc(counted, 1)
            pe.wait_ge(made, CONSTANTS)
            pe.wait_ge(started_ready, 1)
            for h in range(2):
                last = te.matmul(banks[:, TURN + h, 0:HALF], ones_b[0:BLOCKS, :],
                                 started[0:BLOCKS, h * HALF:(h + 1) * HALF], start=True, stop=True)
            last.then_inc(spread, 1)
            for h in range(2):
                te.matmul(banks[:, AGG + h, 0:HALF], minus_block[0:BLOCKS, :],
                          started[0:BLOCKS, h * HALF:(h + 1) * HALF], start=True, stop=False,
                          skip_group_check=True)
            for c in range(CHUNKS):
                pe.wait_ge(at_tile_ready, c + 1)
                if c == 0:
                    pe.wait_ge(split_ready, 2)
                for h in range(2):
                    a, z = chunk_columns(c, h)
                    for part in (dst_high, dst_low) if a < z else ():
                        last = te.matmul(banks[:, AGG + h, a - h * HALF:z - h * HALF], part[:, c * P:(c + 1) * P],
                                         at_tile[c % 2][:, a:z], start=False, stop=False, skip_group_check=True)
                last.then_inc(rel_summed, 1)
            pe.wait_ge(node_idx_ready, len(SOURCE_LOTS))
            turn_sources(typ_f, typ_ready, typ_turned)
            pe.wait_ge(weights_in, 64)
            pe.wait_ge(rel_idx_ready, len(SOURCE_LOTS))
            for n in range(4):
                for k in range(KC):
                    for o in range(KC):
                        last = te.transpose(banks[:, REL + n, (k * KC + o) * P:(k * KC + o + 1) * P],
                                            w_in[n][:, o, k * P:(k + 1) * P], ident[:, :])
                last.then_inc(weights_turned, 1)
            pe.wait_ge(weights_ready, 4)
            pe.wait_ge(biases_in, 32)
            pe.wait_ge(bounds_ready, 1)
            pe.wait_ge(rel_dst_ready, 1)
            pe.sem_inc(m_free, M_SLOTS - 1)

            for n in range(SAGE + 1):
                before = n * BLOCKS
                wl, wr = (wT[0], wT[1]) if n == 0 else (wT[2], wT[3])
                bias = biases[0:1, min(n, 1), :]

                def visit(turn_, k, b, place, hi):
                    parity = place % 2
                    pe.wait_ge(m_ready, turn_ * RING + b + (k + n * VISITS + 1))
                    pe.wait_ge(g_in[k], turn_ * (16 * QUAD) + 16 * QUAD * (n * FILLS[k // RUN] + 1))
                    width = D + (n == 0)

                    def product(i):
                        return te.matmul(banks[:, AGG + (parity + before) % 2, 0:width],
                                         M[:, (k + place + n * VISITS) % M_SLOTS, i, :], G[:, k * QUAD + i, 0:width],
                                         start=False, stop=False, skip_group_check=True)

                    product(0).then_inc(m_free, 1)
                    for i in range(1, QUAD - 1):
                        product(i)
                    with te.If(turn_ * RING + k == hi):
                        product(QUAD - 1).then_inc(agg_done, 1)
                    with te.Else():
                        product(QUAD - 1).then_inc(quad_free, 1)

                def visits(b, place):
                    lo = te.value_load(bounds[0:1, ds(b, 1)], min_val=0, max_val=QUADS - 1)
                    hi = te.value_load(bounds[0:1, ds(b + 1, 1)], min_val=0, max_val=QUADS - 1)
                    if n > 0 or not isinstance(b, int) or b >= 2:
                        pe.wait_ge(agg_read, b + (before - 1))
                    te.matmul(banks[:, AGG + (place + before) % 2, 0:D + (n == 0)], zrow[0:1, 0:P],
                              zrow[0:1, 0:D + (n == 0)], start=True, stop=False, skip_group_check=True)
                    with pe.Fori(lo >> RING_SHIFT, (hi >> RING_SHIFT) + 1) as turn_:
                        for k in range(RING):
                            quad = turn_ * RING + k
                            with te.If((quad - lo) * (hi - quad) >= 0):
                                visit(turn_, k, b, place, hi)

                def turn(j, parity):
                    pe.wait_ge(agg_read, j + (before + 1))
                    if n > 0 or not isinstance(j, int) or j > 0:
                        pe.wait_ge(turn_read, j + before)
                    for k in range(KC):
                        te.transpose(banks[:, TURN, k * P:(k + 1) * P], mean[:, k * P:(k + 1) * P], ident[:, :])
                    for k in range(KC):
                        last = te.transpose(banks[:, TURN, (KC + k) * P:(KC + k + 1) * P],
                                            h_now[:, k * P:(k + 1) * P], ident[:, :])
                    last.then_inc(turn_done, 1)

                def linear(j, parity):
                    pe.wait_ge(turn_read, j + (before + 1))
                    if n > 0 or not isinstance(j, int) or j > 0:
                        pe.wait_ge(lin_read, j + before)
                    te.matmul(banks[:, LIN, 0:D], ones[0:1, :], bias, start=True, stop=False)
                    for k in range(2 * KC):
                        last = te.matmul(banks[:, LIN, 0:D], turned[:, k, :], (wl, wr)[k // KC][:, k % KC, :],
                                         start=False, stop=(k == 2 * KC - 1))
                    last.then_inc(lin_done, 1)

                def turn_h(j, parity):
                    pe.wait_ge(lin_read, j + (before + 1))
                    if not is_first(j):
                        pe.wait_ge(hT_ready, j)
                    for k in range(KC):
                        last = te.transpose(banks[:, REL, k * P:(k + 1) * P], h_next[:, k * P:(k + 1) * P], ident[:, :])
                    last.then_inc(hT_done, 1)

                def project(j, parity):
                    pe.wait_ge(hT_ready, j + 1)
                    if not is_first(j):
                        pe.wait_ge(left_taken, j)
                        pe.wait_ge(root_kept, j)
                    for k in range(KC):
                        te.matmul(banks[:, REL + 1, 0:D], hT[:, k, :], wT[2][:, k, :],
                                  start=(k == 0), stop=(k == KC - 1))
                    te.matmul(banks[:, REL + 2, 0:D], ones[0:1, :], biases[0:1, 1, :], start=True, stop=False)
                    for k in range(KC):
                        last = te.matmul(banks[:, REL + 2, 0:D], hT[:, k, :], wT[3][:, k, :],
                                         start=False, stop=(k == KC - 1))
                    last.then_inc(projected, 1)

                def turn_x1(j, parity):
                    pe.wait_ge(x1_ready, j + 1)
                    if is_first(j):
                        pe.wait_ge(turn_read, (SAGE - 1) * BLOCKS)
                    else:
                        pe.wait_ge(x1T_ready, j)
                    for k in range(KC):
                        last = te.transpose(banks[:, TURN, k * P:(k + 1) * P], x1_now[:, k * P:(k + 1) * P],
                                            ident[:, :])
                    last.then_inc(x1_turned, 1)

                def relations(j, parity):
                    pe.wait_ge(x1T_ready, j + 1)
                    for q in range(4):
                        if q % 2 == 0 and not is_first(j):
                            pe.wait_ge((low_taken, high_taken)[q // 2], j)
                        for k in range(KC):
                            last = te.matmul(banks[:, REL + q, :], x1T[:, k, :], wrel[:, k, q * 512:(q + 1) * 512],
                                             start=(k == 0), stop=(k == KC - 1))
                        if q % 2 == 1:
                            last.then_inc(rel_done, 1)

                def sum_first(j, parity):
                    if isinstance(j, int) and j == 0:
                        pe.wait_ge(first_copied, 1)
                        te.matmul(banks[:, TURN, 0:D], ones[:, :], mean[:, :], start=True,
                                  stop=True).then_inc(first_summed, 1)

                def sums(j, place):
                    rows = LAST_ROWS if isinstance(j, int) and j == BLOCKS - 1 else P
                    pe.wait_ge(agg_read, j + (before + 1))
                    pe.wait_ge(sq_ready, j + 1)
                    te.matmul(banks[:, LIN, 0:D], ones[0:rows, :], H[0:rows, j, :],
                              start=False, stop=False, skip_group_check=True)
                    te.matmul(banks[:, LIN, D:2 * D], ones[0:rows, :], square[0:rows, place % 2, :],
                              start=False, stop=False, skip_group_check=True).then_inc(sums_done, 1)

                if n == 0:
                    over_blocks(pe, [(0, visits), (1, turn), (1, linear)], unroll=M_SLOTS)
                elif n == 1:
                    over_blocks(pe, [(0, visits), (2, turn_h), (1, turn), (2, project), (1, linear)], unroll=M_SLOTS)
                elif n == 2:
                    pe.wait_ge(wrel_in, 16 * KC)
                    over_blocks(pe, [(0, visits), (1, relations), (0, turn_x1)], unroll=M_SLOTS)
                else:
                    pe.wait_ge(lin_read, (SAGE - 1) * BLOCKS)
                    te.matmul(banks[:, LIN, 0:2 * D], zrow[0:1, 0:P], zrow[0:1, :],
                              start=True, stop=False, skip_group_check=True)
                    over_blocks(pe, [(0, visits), (0, sum_first), (1, sums)], unroll=M_SLOTS)

            pe.wait_ge(offset_ready, 1)
            for i, g in enumerate(BY_TENSOR):
                if i >= 2:
                    pe.wait_ge(z_ready, BY_TENSOR[i - 2] + 1)
                for j in range(GROUP):
                    to = banks[:, i % 2 * 4 + j // 2, j % 2 * D:(j % 2 + 1) * D]
                    te.matmul(to, ident[:, :], X[:, g * GROUP + j, :], start=True, stop=False)
                    last = te.matmul(to, ones[0:1, :], shift[0:1, :], start=False, stop=True)
                last.then_inc(offset_in_banks, 1)

        @block.vector
        def _(dve):
            ve = nc.vector
            def take_sources(turned_, idx, ready):
                for k, (c0, c1) in enumerate(SOURCE_LOTS):
                    dve.wait_ge(turned_, k + 1)
                    ve.tensor_copy(idx[:, c0 * P:c1 * P], banks[:, REL + k, 0:(c1 - c0) * P]).then_inc(ready, 1)

            dve.wait_ge(src_in, 16 * 3)
            ve.tensor_copy(src_f, src_i).then_inc(src_ready, 1)
            dve.wait_ge(dst_in, 16 * 3)
            ve.tensor_copy(dst_f, dst_i).then_inc(dst_ready, 1)
            take_sources(src_turned, node_idx, node_idx_ready)
            dve.wait_ge(made, 4)
            ve.tensor_scalar(fourth_i, fourth_i, QUAD - 1, None, ALU.bitwise_and).then_inc(fourth_ready, 1)
            dve.wait_ge(fourth_ready, 1)
            ve.tensor_scalar(fourth, fourth_i, float(QUAD - 1), None, ALU.is_equal).then_inc(fourth_ready, 1)
            dve.wait_ge(dst_ready, 1)
            for c in range(CHUNKS):
                ve.tensor_scalar(below[:, c * 64:(c + 1) * 64], thresholds, dst_f[:, (c + 1) * P - 1:(c + 1) * P],
                                 None, ALU.is_gt).then_inc(below_ready, 1)
            ve.tensor_scalar(dst_low_i, dst_i, 255, None, ALU.bitwise_and).then_inc(low_ready, 1)
            dve.wait_ge(low_ready, 1)
            ve.tensor_copy(dst_low, dst_low_i).then_inc(split_ready, 1)
            dve.wait_ge(split_ready, 1)
            ve.tensor_tensor(dst_high, dst_f, dst_low, ALU.subtract).then_inc(split_ready, 1)
            dve.wait_ge(counted, 1)
            ve.tensor_tensor(first_visit[0:BOUNDS, :], banks[0:BOUNDS, AGG, 0:1], part_iota[0:BOUNDS, :],
                             ALU.add).then_inc(first_ready, 1)
            ve.tensor_copy(bounds[0:1, :], banks[0:1, AGG + 1, 0:BOUNDS]).then_inc(bounds_ready, 1)
            dve.wait_ge(first_ready, 1)
            dve.wait_ge(made, CONSTANTS)
            ve.tensor_scalar(started[0:BLOCKS, :], visit_iota[0:BLOCKS, :], first_visit[0:BLOCKS, :],
                             None, ALU.is_ge).then_inc(started_ready, 1)
            dve.wait_ge(typ_in, 16 * 3)
            ve.scalar_tensor_tensor(out=typ_f, in0=src_i, scalar=float(RELS), in1=typ_i,
                                    op0=ALU.mult, op1=ALU.add).then_inc(typ_ready, 1)

            dve.wait_ge(spread, 1)
            for h in range(2):
                ve.scalar_tensor_tensor(out=tile_of[:, h * HALF:(h + 1) * HALF], in0=banks[:, TURN + h, 0:HALF],
                                        scalar=-float(QUAD), in1=column_iota[:, h * HALF:(h + 1) * HALF],
                                        op0=ALU.mult, op1=ALU.add).then_inc(tile_of_ready, 1)
            dve.wait_ge(tile_of_ready, 2)
            for c in range(CHUNKS):
                if c >= 2:
                    dve.wait_ge(rel_summed, c - 1)
                a, z = chunk_columns(c)
                ve.tensor_scalar(at_tile[c % 2][:, a:z], tile_of[:, a:z], tile_iota[:, c:c + 1], None,
                                 ALU.is_equal).then_inc(at_tile_ready, 1)
            dve.wait_ge(rel_summed, CHUNKS)
            for h in range(2):
                last = ve.tensor_copy(rel_dst[:, h * HALF:(h + 1) * HALF], banks[:, AGG + h, 0:HALF])
            last.then_inc(rel_dst_ready, 1)
            take_sources(typ_turned, rel_idx, rel_idx_ready)
            dve.wait_ge(rel_dst_ready, 1)
            dve.wait_ge(bounds_ready, 1)

            for n in range(SAGE + 1):
                before = n * BLOCKS

                def selections(b, parity):
                    lo = ve.value_load(bounds[0:1, ds(b, 1)], min_val=0, max_val=QUADS - 1)
                    hi = ve.value_load(bounds[0:1, ds(b + 1, 1)], min_val=0, max_val=QUADS - 1)
                    with dve.Fori(lo, hi + 1) as quad:
                        dve.wait_ge(m_free, quad + b + (n * VISITS + 1))
                        ve.tensor_tensor(
                            M[:, (quad + b + n * VISITS) & (M_SLOTS - 1), :, :],
                            node_iota[:, :].unsqueeze(1).to_broadcast([P, QUAD, P]),
                            rel_dst[:, ds((quad + b) * QUAD, QUAD)].unsqueeze(2).to_broadcast([P, QUAD, P]),
                            ALU.is_equal).then_inc(m_ready, 1)

                def degrees(j, parity):
                    dve.wait_ge(agg_done, j + 1)
                    ve.tensor_scalar(rdeg[:, ds(j, 1)], banks[:, AGG + parity, D:D + 1], 1.0, None,
                                     ALU.max).then_inc(deg_clamped, 1)
                    wait_apart(dve, deg_clamped, j + 1)
                    ve.reciprocal(rdeg[:, ds(j, 1)], rdeg[:, ds(j, 1)]).then_inc(deg_ready, 1)

                def keep_root(j, parity):
                    dve.wait_ge(projected, j + 1)
                    ve.tensor_tensor(H[:, j, :], banks[:, REL + 2, 0:D], X[:, j, :], ALU.add).then_inc(root_kept, 1)

                def layernorm(j, parity):
                    dve.wait_ge(agg_done, j + (before + 1))
                    if not isinstance(j, int) or j > 0:
                        dve.wait_ge(x1_turned, j)
                        dve.wait_ge(x1_kept, j)
                    ve.scalar_tensor_tensor(out=x1_now[:, :], in0=banks[:, AGG + (parity + before) % 2, 0:D],
                                            scalar=rdeg[:, ds(j, 1)], in1=H[:, j, :], op0=ALU.mult,
                                            op1=ALU.add).then_inc(agg_read, 1)
                    dve.wait_ge(agg_read, j + (before + 1))
                    ve.bn_stats(stats[:, 0, :], x1_now[:, :]).then_inc(y_stats, 1)
                    wait_apart(dve, y_stats, j + 1)
                    ve.bn_aggr(moments[:, 0, :], stats[:, 0, :]).then_inc(y_moments, 1)
                    dve.wait_ge(y_root, j + 1)
                    ve.reciprocal(rstd[:, 0, 0:1], rstd[:, 0, 0:1]).then_inc(y_rstd, 1)
                    dve.wait_ge(y_rstd, j + 1)
                    ve.tensor_scalar(x1_now[:, :], x1_now[:, :], moments[:, 0, 0:1], rstd[:, 0, 0:1], ALU.subtract,
                                     ALU.mult).then_inc(x1_ready, 1)

                def take_high(j, parity):
                    if not isinstance(j, int) or j >= 2:
                        dve.wait_ge(rel_out[parity], (j - parity) * 8)
                    dve.wait_ge(rel_done, j * 2 + 2)
                    ve.tensor_copy(stage[:, parity, HALF_RELS * D:].rearrange("p (q c) -> p q c", q=2),
                                   banks[:, REL + 2:REL + 4, :]).then_inc(high_taken, 1)

                def deviations(j, parity):
                    bank = AGG + (parity + before) % 2
                    dve.wait_ge(agg_done, j + (before + 1))
                    if isinstance(j, int) and j == 0:
                        ve.tensor_copy(mean[:, :], banks[:, bank, 0:D]).then_inc(first_copied, 1)
                        dve.wait_ge(first_summed, 1)
                        ve.tensor_scalar(shift, banks[:, TURN, 0:D], 1.0 / P, None, ALU.mult).then_inc(shift_ready, 1)
                        dve.wait_ge(shift_ready, 1)
                    ve.tensor_tensor(H[:, j, :], banks[:, bank, 0:D], shift, ALU.subtract).then_inc(agg_read, 1)

                if n == 0:
                    over_blocks(dve, [(0, selections), (0, degrees)])
                elif n == 1:
                    over_blocks(dve, [(0, selections), (3, keep_root)])
                elif n == 2:
                    over_blocks(dve, [(0, selections), (2, take_high), (0, layernorm)], peel=2)
                else:
                    over_blocks(dve, [(0, selections), (0, deviations)])

            steps = [0]

            def then(ins):
                steps[0] += 1
                ins.then_inc(bn_step, 1)
                dve.wait_ge(bn_step, steps[0])

            dve.wait_ge(norm_in, 32)
            dve.wait_ge(sums_done, BLOCKS)
            then(ve.tensor_scalar(mean[:, 0:D], banks[:, LIN, 0:D], 1.0 / N_NODES, None, ALU.mult))
            then(ve.tensor_tensor(shift, mean[:, 0:D], mean[:, 0:D], ALU.mult))
            then(ve.scalar_tensor_tensor(out=scale_b, in0=banks[:, LIN, D:2 * D], scalar=1.0 / N_NODES,
                                         in1=shift, op0=ALU.mult, op1=ALU.subtract))
            dve.wait_ge(bn_root, 1)
            then(ve.reciprocal(scale_b, scale_b))
            then(ve.tensor_tensor(scale_b, scale_b, gamma_b, ALU.mult))
            ve.tensor_tensor(mean[:, 0:D], mean[:, 0:D], scale_b, ALU.mult).then_inc(scale_ready, 1)
            dve.wait_ge(scale_ready, 1)
            ve.tensor_tensor(shift, beta_b, mean[:, 0:D], ALU.subtract).then_inc(offset_ready, 1)
            dve.wait_ge(offset_ready, 1)
            def factors(g):
                of_group = rstd[:, g % 2, :]
                dve.wait_ge(z_root, g + 1)
                ve.reciprocal(of_group, of_group).then_inc(z_rstd, 1)
                dve.wait_ge(z_rstd, g + 1)
                ve.scalar_tensor_tensor(out=nbias[:, g % 2, :], in0=moments[:, :, 0], scalar=-1.0, in1=of_group,
                                        op0=ALU.mult, op1=ALU.mult).then_inc(norm_ready, 1)

            for g in range(GROUPS):
                b0 = g * GROUP
                xg, zg = X[:, b0:b0 + GROUP, :], H[:, b0:b0 + GROUP, :]
                if g in BY_TENSOR:
                    dve.wait_ge(offset_in_banks, BY_TENSOR.index(g) + 1)
                    half = BY_TENSOR.index(g) % 2 * 4
                    xg = banks[:, half:half + 4, :].rearrange("p q (r d) -> p (q r) d", r=2)[:, 0:GROUP, :]
                elif g in BY_POOL:
                    dve.wait_ge(offset_by_pool, BY_POOL.index(g) + 1)
                else:
                    ve.tensor_tensor(xg, xg, shift.unsqueeze(1).to_broadcast([P, GROUP, D]),
                                     ALU.add).then_inc(offset_added, 1)
                    dve.wait_ge(offset_added, g + 1)
                if g == 0:
                    ve.tensor_tensor(zg, zg, scale_b.unsqueeze(1).to_broadcast([P, GROUP, D]),
                                     ALU.mult).then_inc(first_scaled, 1)
                    dve.wait_ge(first_scaled, 1)
                else:
                    dve.wait_ge(scaled, g)
                ve.tensor_tensor(zg, zg, xg, ALU.add).then_inc(z_ready, 1)
                if g > 0:
                    if g > 2:
                        dve.wait_ge(normed, (g - 2) * GROUP)
                    factors(g - 1)
                dve.wait_ge(z_ready, g + 1)
                for i in range(GROUP):
                    ve.bn_stats(stats[:, i, :], H[:, b0 + i, :]).then_inc(z_stats, 1)
                dve.wait_ge(z_stats, b0 + GROUP)
                if g > 0:
                    dve.wait_ge(norm_ready, g)
                for i in range(GROUP):
                    ve.bn_aggr(moments[:, i, :], stats[:, i, :]).then_inc(z_moments, 1)
            factors(GROUPS - 1)

        @block.scalar
        def _(act):
            sc = nc.scalar
            for n in range(4):
                act.wait_ge(weights_turned, n + 1)
                sc.activation(wT[n][:, :, :], banks[:, REL + n, :].rearrange("p (k o) -> p k o", k=KC),
                              ACT.Copy).then_inc(weights_ready, 1)
            for n in range(SAGE + 1):
                before = n * BLOCKS

                def means(j, parity):
                    act.wait_ge(agg_done, j + (before + 1))
                    if n == 0:
                        act.wait_ge(deg_ready, j + 1)
                    if n > 0 or not isinstance(j, int) or j > 0:
                        act.wait_ge(turn_done, j + before)
                    if n == 0 and is_first(j):
                        act.wait_ge(x_in[0], 16)
                    elif n == 0 and isinstance(j, int) and j == GROUP - 1:
                        for g in range(1, GROUPS):
                            act.wait_ge(x_in[g], 16 if g < GROUPS - 1 else 32)
                    sc.activation(h_now[:, :], (X if n == 0 else H)[:, j, :], ACT.Copy)
                    sc.activation(mean[:, :], banks[:, AGG + (parity + before) % 2, 0:D], ACT.Copy,
                                  scale=rdeg[:, ds(j, 1)]).then_inc(agg_read, 1)

                def take_turned(j, parity):
                    act.wait_ge(turn_done, j + (before + 1))
                    if n > 0 or not isinstance(j, int) or j > 0:
                        act.wait_ge(lin_done, j + before)
                    sc.activation(turned[:, :, :], banks[:, TURN, :].rearrange("p (k m) -> p k m", m=P),
                                  ACT.Copy).then_inc(turn_read, 1)

                def hidden(j, parity):
                    wait_apart(act, lin_done, j + (before + 1))
                    if n == 0:
                        sc.activation(H[:, j, :], banks[:, LIN, 0:D], ACT.Relu).then_inc(lin_read, 1)
                    else:
                        if not is_first(j):
                            act.wait_ge(hT_done, j)
                        sc.activation(h_next[:, :], banks[:, LIN, 0:D], ACT.Relu).then_inc(lin_read, 1)

                def write_h(j, parity):
                    act.wait_ge(lin_read, j + 1)
                    act.dma_start(tables[1][ds(j * P, P), :], H[:, j, :]).then_inc(table_out[parity], 16)

                def take_hT(j, parity):
                    act.wait_ge(hT_done, j + 1)
                    if not is_first(j):
                        act.wait_ge(projected, j)
                    sc.activation(hT[:, :, :], banks[:, REL, 0:D].rearrange("p (k m) -> p k m", m=P),
                                  ACT.Copy).then_inc(hT_ready, 1)

                def take_left(j, parity):
                    if isinstance(j, int) and j < 2:
                        act.wait_ge(weights_turned, 4)
                    else:
                        act.wait_ge(table_out[parity], (j - parity) * 8 + 16 * ((BLOCKS + 1 - parity) // 2))
                    act.wait_ge(projected, j + 1)
                    sc.activation(stage[:, parity, 0:D], banks[:, REL + 1, 0:D], ACT.Copy).then_inc(left_taken, 1)

                def write_left(j, parity):
                    act.wait_ge(left_taken, j + 1)
                    act.dma_start(tables[2][ds(j * P, P), :], stage[:, parity, 0:D]).then_inc(table_out[parity], 16)

                def write_relations(j, parity):
                    act.wait_ge(low_taken, j + 1)
                    act.wait_ge(high_taken, j + 1)
                    act.dma_start(rel_table[ds(j * P * RELS, P * RELS), :].rearrange("(p r) c -> p (r c)", r=RELS),
                                  stage[:, parity, :]).then_inc(rel_out[parity], 16)

                def root(j, parity):
                    act.wait_ge(y_moments, j + 1)
                    if not isinstance(j, int) or j > 0:
                        act.wait_ge(x1_ready, j)
                    sc.activation(rstd[:, 0, 0:1], moments[:, 0, 1:2], ACT.Sqrt, bias=eps[:, :]).then_inc(y_root, 1)

                def keep_x1(j, parity):
                    act.wait_ge(x1_ready, j + 1)
                    sc.activation(X[:, j, :], x1_now[:, :], ACT.Copy).then_inc(x1_kept, 1)

                def take_x1T(j, parity):
                    act.wait_ge(x1_turned, j + 1)
                    if not isinstance(j, int) or j > 0:
                        act.wait_ge(rel_done, j)
                    sc.activation(x1T[:, :, :], banks[:, TURN, 0:D].rearrange("p (k m) -> p k m", m=P),
                                  ACT.Copy).then_inc(x1T_ready, 1)

                def take_low(j, parity):
                    if isinstance(j, int) and j < 2:
                        act.wait_ge(table_out[parity], 2 * 16 * ((BLOCKS + 1 - parity) // 2))
                    else:
                        act.wait_ge(rel_out[parity], (j - parity) * 8)
                    act.wait_ge(rel_done, j * 2 + 1)
                    sc.activation(stage[:, parity, 0:HALF_RELS * D].rearrange("p (q c) -> p q c", q=2),
                                  banks[:, REL:REL + 2, :], ACT.Copy).then_inc(low_taken, 1)

                def squares(j, parity):
                    act.wait_ge(agg_read, j + (before + 1))
                    if not isinstance(j, int) or j >= 2:
                        act.wait_ge(sums_done, j - 1)
                    sc.activation(square[:, parity, :], H[:, j, :], ACT.Square).then_inc(sq_ready, 1)

                if n == 0:
                    over_blocks(act, [(1, take_turned), (0, means), (1, hidden), (1, write_h)], peel=GROUP)
                elif n == 1:
                    over_blocks(act, [(2, take_hT), (1, take_turned), (0, means), (2, take_left), (1, hidden),
                                      (2, write_left)])
                elif n == 2:
                    over_blocks(act, [(0, root), (2, write_relations), (0, keep_x1), (1, take_low), (0, take_x1T)])
                else:
                    over_blocks(act, [(0, squares)], peel=2)

            act.wait_ge(bn_step, 3)
            sc.activation(scale_b, scale_b, ACT.Sqrt, bias=eps[:, :]).then_inc(bn_root, 1)
            for g in range(GROUPS):
                act.wait_ge(z_moments, (g + 1) * GROUP)
                sc.activation(rstd[:, g % 2, :], moments[:, :, 1], ACT.Sqrt, bias=eps[:, :]).then_inc(z_root, 1)
                act.wait_ge(norm_ready, g + 1)
                for i in range(GROUP):
                    zb = H[:, g * GROUP + i, :]
                    sc.activation(zb, zb, ACT.Identity, scale=rstd[:, g % 2, i:i + 1],
                                  bias=nbias[:, g % 2, i:i + 1]).then_inc(normed, 1)


_INS = ['x', 'src', 'dst', 'edge_type_8', 'L0_gnn_W1l', 'L0_gnn_b1l', 'L0_gnn_W1r', 'L0_gnn_W2l', 'L0_gnn_b2l',
        'L0_gnn_W2r', 'L1_gnn_weight', 'L1_gnn_gamma', 'L1_gnn_beta']
_OUT = ((N_NODES, D), 'float32')


def kernel(**inputs):
    import concourse.bacc as _bacc
    from concourse.bass_utils import run_bass_kernel_spmd as _run

    nc = _bacc.Bacc("TRN2", target_bir_lowering=False, num_devices=1)
    arrays, args = {}, []
    for name in _INS:
        a = np.ascontiguousarray(inputs[name])
        arrays[f"in_{name}"] = a
        args.append(nc.dram_tensor(f"in_{name}", a.shape, mybir.dt.from_np(a.dtype), kind="ExternalInput").ap())
    args.append(nc.dram_tensor("result", _OUT[0], mybir.dt.from_np(np.dtype(_OUT[1])), kind="ExternalOutput").ap())
    build_gnn(nc, *args)
    return _run(nc, [arrays], core_ids=[0]).results[0]["result"]
```
